# Optimizing a Trainium2 kernel written in Bass

```python
import numpy as np
import jax
import jax.numpy as jnp

def _softmax(x, axis=-1):
    return jax.nn.softmax(x, axis=axis)

def _gelu(x):
    return jax.nn.gelu(x, approximate=True)

def _silu(x):
    return jax.nn.silu(x)

def _sigmoid(x):
    return jax.nn.sigmoid(x)

def _layernorm(x, axis=-1, eps=1e-05):
    m = jnp.mean(x, axis=axis, keepdims=True)
    v = jnp.var(x, axis=axis, keepdims=True)
    return (x - m) / jnp.sqrt(v + eps)

def _scatter_add(tgt, idx, src, axis=0):
    return tgt.at[idx].add(src)

def _segment_sum(src, seg, n):
    return jax.ops.segment_sum(src, seg, n)
kernel_name = 'mk_seq_preln_d1_jaxref_r8_476f52'

def setup_inputs(seed: int=0):
    np.random.seed(seed)
    _w = jnp.asarray

    def _L0_attn_setup():
        import jax, jax.numpy as jnp
        import numpy as np
        D_MODEL = 256
        GN_EPS = 1e-05
        key = jax.random.key(seed)
        ks = jax.random.split(key, 6)
        B, T, D = (4, 256, D_MODEL)
        s = 1.0 / np.sqrt(D)
        return {'x': jax.random.normal(ks[0], (B, T, D), dtype=jnp.float32), 'Wr': jax.random.normal(ks[1], (D, D), dtype=jnp.float32) * s, 'Wk': jax.random.normal(ks[2], (D, D), dtype=jnp.float32) * s, 'Wv': jax.random.normal(ks[3], (D, D), dtype=jnp.float32) * s, 'Wo': jax.random.normal(ks[4], (D, D), dtype=jnp.float32) * s, 'decay': jnp.ones((D,), dtype=jnp.float32) * 0.99, 'gn_weight': jnp.ones((D,), dtype=jnp.float32), 'gn_bias': jnp.zeros((D,), dtype=jnp.float32)}
    _L0_attn_in = _L0_attn_setup()

    def _L0_ffn_setup():
        import jax, jax.numpy as jnp
        import numpy as np
        B, S, D, H = (8, 512, 256, 640)

        def ternarize_weight(w):
            abs_mean = jnp.maximum(jnp.mean(jnp.abs(w)), 1e-05)
            thr = 0.7 * abs_mean
            one = jnp.ones((), dtype=w.dtype)
            q = jnp.where(w > thr, one, jnp.where(w < -thr, -one, jnp.zeros((), dtype=w.dtype)))
            return w + jax.lax.stop_gradient(q * abs_mean - w)
        key = jax.random.key(seed)
        k1, k2, k3 = jax.random.split(key, 3)
        x = jax.random.normal(k1, (B, S, D), dtype=jnp.float32)
        w_fc = jax.random.normal(k2, (H, D), dtype=jnp.float32) / np.sqrt(D).astype(np.float32)
        w_proj = jax.random.normal(k3, (D, H), dtype=jnp.float32) / np.sqrt(H).astype(np.float32)
        return {'x': x, 'w_fc': w_fc, 'w_proj': w_proj}
    _L0_ffn_in = _L0_ffn_setup()
    _d = {'L0_attn_x': _L0_attn_in['x'], 'L0_attn_Wr': _L0_attn_in['Wr'], 'L0_attn_Wk': _L0_attn_in['Wk'], 'L0_attn_Wv': _L0_attn_in['Wv'], 'L0_attn_Wo': _L0_attn_in['Wo'], 'L0_attn_decay': _L0_attn_in['decay'], 'L0_attn_gn_weight': _L0_attn_in['gn_weight'], 'L0_attn_gn_bias': _L0_attn_in['gn_bias'], 'L0_ffn_w_fc': _L0_ffn_in['w_fc'], 'L0_ffn_w_proj': _L0_ffn_in['w_proj']}
    _x0 = _d['L0_attn_x']
    _d['L0_attn_x'] = jax.random.normal(jax.random.fold_in(jax.random.key(seed), 1), (8, 256, 256), dtype=_x0.dtype)
    del _x0
    return _d

def reference(L0_attn_x, L0_attn_Wr, L0_attn_Wk, L0_attn_Wv, L0_attn_Wo, L0_attn_decay, L0_attn_gn_weight, L0_attn_gn_bias, L0_ffn_w_fc, L0_ffn_w_proj):

    def _L0_attn_ref(x, Wr, Wk, Wv, Wo, decay, gn_weight, gn_bias):
        import jax, jax.numpy as jnp
        import numpy as np
        D_MODEL = 256
        GN_EPS = 1e-05
        B, T, D = x.shape
        r = jax.nn.sigmoid(jnp.einsum('btd,ed->bte', x, Wr))
        k = jnp.einsum('btd,ed->bte', x, Wk)
        v = jnp.einsum('btd,ed->bte', x, Wv)
        d = jax.nn.sigmoid(decay)
        log_decay = jnp.log(jnp.clip(d, 1e-07, None))
        pos = jnp.arange(T, dtype=x.dtype)
        scale = jnp.exp(pos[:, None] * log_decay[None, :])
        scaled = k * v / jnp.clip(scale, 1e-10, None)[None]
        state = jnp.cumsum(scaled, axis=1) * scale[None]
        out = r * state
        mean = jnp.mean(out, axis=(1, 2), keepdims=True)
        var = jnp.mean(jnp.square(out - mean), axis=(1, 2), keepdims=True)
        normed = (out - mean) * jax.lax.rsqrt(var + GN_EPS)
        normed = normed * gn_weight + gn_bias
        return jnp.einsum('btd,ed->bte', normed, Wo)

    def _L0_ffn_ref(x, w_fc, w_proj):
        import jax, jax.numpy as jnp
        import numpy as np
        B, S, D, H = (8, 512, 256, 640)

        def ternarize_weight(w):
            abs_mean = jnp.maximum(jnp.mean(jnp.abs(w)), 1e-05)
            thr = 0.7 * abs_mean
            one = jnp.ones((), dtype=w.dtype)
            q = jnp.where(w > thr, one, jnp.where(w < -thr, -one, jnp.zeros((), dtype=w.dtype)))
            return w + jax.lax.stop_gradient(q * abs_mean - w)
        h = jnp.einsum('bsd,hd->bsh', x, ternarize_weight(w_fc))
        h = jnp.square(jax.nn.relu(h))
        return jnp.einsum('bsh,dh->bsd', h, ternarize_weight(w_proj))
    x = L0_attn_x
    x = x + _L0_attn_ref(_layernorm(x, axis=-1), L0_attn_Wr, L0_attn_Wk, L0_attn_Wv, L0_attn_Wo, L0_attn_decay, L0_attn_gn_weight, L0_attn_gn_bias)
    x = x + _L0_ffn_ref(_layernorm(x, axis=-1), L0_ffn_w_fc, L0_ffn_w_proj)
    return x

_drawn_inputs = setup_inputs


def setup_inputs(seed=0):
    import zlib

    import numpy as np

    out = dict(_drawn_inputs(seed))
    spreads = {'L0_attn_decay': (0.9900000095367432, 0.2),
     'L0_attn_gn_weight': (1.0, 0.2),
     'L0_attn_gn_bias': (0.0, 0.1)}
    factors = {}
    for name, (base, spread) in spreads.items():
        noise = np.random.default_rng([zlib.crc32(name.encode()), seed]).standard_normal(out[name].shape)
        drawn = base * np.exp(spread * noise) if base else spread * noise
        out[name] = jnp.asarray(drawn.astype(out[name].dtype))
    for name, factor in factors.items():
        out[name] = (out[name] * factor).astype(out[name].dtype)
    return out
```

```python
import numpy as np
import concourse.bass as bass
from concourse import mybir
from contextlib import ExitStack

P = 128


def decay_block_kernel(nc, x, w_qkv, w_out, columns, w_fc, w_proj, out):
    F32, F16, U32 = mybir.dt.float32, mybir.dt.float16, mybir.dt.uint32
    ALU, ACT, AX = mybir.AluOpType, mybir.ActivationFunctionType, mybir.AxisListType

    D = 256
    NB = 8
    T = x.shape[1] // NB // D * P
    CD, CT = D // P, T // P
    N = CT * D
    H = w_fc.shape[1] // CD
    CH = H // P
    assert T == D and N == 512
    EPS = 1e-5
    EXPONENT = 0x7F800000

    X_SCALE = 2.0 ** 8
    Z_SCALE = 2.0 ** 7
    W_SCALE = 2.0 ** 14
    H_SCALE = 2.0 ** -1
    LAST = NB - 1
    LOOP = (3, NB - 1)
    SLOTS = NB + 3

    PAIRS = [(0, 2), (2, 4), (4, CH)]

    ctx = ExitStack()
    with ctx:
        def sb(name, shape, dt):
            return ctx.enter_context(nc.sbuf_tensor(name, shape, dt))

        def sem(name):
            return ctx.enter_context(nc.semaphore(name))

        wait_taker = sb("wait_taker", [P, 1], F32)
        ident = sb("ident", [P, P], F32)
        ones = sb("ones", [P, P], F32)
        mean_mat = sb("mean_mat", [P, P], F32)
        square_mat = sb("square_mat", [P, P], F32)
        minus_half = sb("minus_half", [P, CT], F32)
        minus_one = sb("minus_one", [P, CT], F32)
        position = sb("position", [P, T], F32)
        cols = sb("cols", [P, 3 * CD], F32)
        decay_c, gn_w_c, gn_b_c = cols[:, 0:CD], cols[:, CD:2 * CD], cols[:, 2 * CD:3 * CD]
        w_raw = sb("w_raw", [P, 4, CD * D], F32)
        w_hi = sb("w_hi", [P, 4, CD * D], F16)
        w_lo = sb("w_lo", [P, 4, CD * D], F16)
        wo_gn = sb("wo_gn", [P, CD * D], F32)
        w_max = sb("w_max", [P, 4], F32)
        w_max_all = sb("w_max_all", [4, 2], F32)
        w_max_diag = sb("w_max_diag", [4, 8], F32)
        w_pow = sb("w_pow", [P, 4], F32)
        w_inv = sb("w_inv", [P, 4], F32)
        w_mul = sb("w_mul", [P, 4], F32)
        unscale = sb("unscale", [P, 4], F32)
        y_unscale = sb("y_unscale", [P, 1], F32)
        d_exp = sb("d_exp", [P, CD], F32)
        d_exp1 = sb("d_exp1", [P, CD], F32)
        d_sig = sb("d_sig", [P, CD], F32)
        d_keep = sb("d_keep", [P, CD], F32)
        d_log = sb("d_log", [P, CD], F32)
        d_scale = sb("d_scale", [P, CD, T], F32)
        d_ratio = sb("d_ratio", [P, CD * T], F32)
        kv_weight = sb("kv_weight", [P, CD * T], F32)
        gnb_wide = sb("gnb_wide", [P, CD, P], F32)
        bias_row = sb("bias_row", [P, D], F32)
        f_raw = sb("f_raw", [P, 2, CD * H], F32)
        f_abs = sb("f_abs", [P, CD * H], F32)
        f_sum = sb("f_sum", [P, 2], F32)
        f_mean = sb("f_mean", [P, 2], F32)
        f_thr = sb("f_thr", [P, 2], F32)
        f_nthr = sb("f_nthr", [P, 2], F32)
        f_neg = sb("f_neg", [P, 2, CD * H], F16)
        f_q = sb("f_q", [P, 2, CD * H], F16)
        f_m2 = sb("f_m2", [P, 1], F32)
        f_unscale = sb("f_unscale", [P, 1], F32)

        x_all = sb("x_all", [P, NB * N], F32)
        ln_stats = [sb(f"ln{n}_stats", [P, CT, 6], F32) for n in (1, 2)]
        ln_mv = [sb(f"ln{n}_mv", [P, CT, 2], F32) for n in (1, 2)]
        ln_var = [sb(f"ln{n}_var", [P, CT], F32) for n in (1, 2)]
        ln_nm = [sb(f"ln{n}_nm", [P, CT], F32) for n in (1, 2)]
        ln_rs = [sb(f"ln{n}_rs", [P, CT], F32) for n in (1, 2)]
        ln_bias = [sb(f"ln{n}_bias", [P, CT], F32) for n in (1, 2)]
        xn = [sb(f"xn{n}", [P, N], F32) for n in (1, 2)]
        xt_hi = [sb(f"xt{n}_hi", [P, CD, T], F16) for n in (1, 2)]
        xt_lo = [sb(f"xt{n}_lo", [P, CD, T], F16) for n in (1, 2)]
        k_sb = sb("k_sb", [P, N], F32)
        kw_sb = sb("kw_sb", [P, N], F32)
        u_sb = sb("u_sb", [P, CD, T], F32)
        state = sb("state", [P, CD, T], F32)
        gate = sb("gate", [P, N], F32)
        o_sb = sb("o_sb", [P, N], F32)
        gn_stats = sb("gn_stats", [P, 6], F32)
        gn_mv = sb("gn_mv", [P, 2], F32)
        gn_sq = sb("gn_sq", [P, 1], F32)
        gn_all = sb("gn_all", [P, 2], F32)
        gn_nvar = sb("gn_nvar", [P, 1], F32)
        gn_nveps = sb("gn_nveps", [P, 1], F32)
        gn_veps = sb("gn_veps", [P, 1], F32)
        gn_nm = sb("gn_nm", [P, 1], F32)
        gn_rs = sb("gn_rs", [P, 1], F32)
        gn_bias = sb("gn_bias", [P, 1], F32)
        z_sb = sb("z_sb", [P, N], F32)
        z_hi = sb("z_hi", [P, CD, T], F16)
        z_lo = sb("z_lo", [P, CD, T], F16)
        h_relu = sb("h_relu", [P, CH * T], F32)
        h_sq = sb("h_sq", [P, CH * T], F32)
        h_hi = sb("h_hi", [P, CH * T], F16)
        h_lo = sb("h_lo", [P, CH * T], F16)
        ffn_out = sb("ffn_out", [P, N], F32)

        bank = [ctx.enter_context(nc.psum_tensor(f"bank_{n}", [P, 512], F32))
                for n in ("turn", "k", "v", "r", "y", "o", "h0", "h1")]
        b_turn, b_k, b_v, b_r, b_y, b_o = bank[:6]
        b_h = [bank[6], bank[7], bank[6]]

        in_x = [sem("in_x0"), sem("in_x1"), sem("in_x_rest")]
        in_wqkv, in_wout, in_cols = sem("in_wqkv"), sem("in_wout"), sem("in_cols")
        in_fc, in_proj, stored = sem("in_fc"), sem("in_proj"), sem("stored")
        consts_step, consts_ready = sem("consts_step"), sem("consts_ready")
        setup_step = sem("setup_step")
        wmax_ready, wmax_turned, wdiag_ready, wmax_spread = sem("wmax_ready"), sem("wmax_turned"), sem("wdiag_ready"), sem("wmax_spread")
        wscale_ready, whi_ready, wlo_ready = sem("wscale_ready"), sem("whi_ready"), sem("wlo_ready")
        dexp_ready, dkeep_ready, dlog_ready, dscale_ready, kvw_ready = sem("dexp_ready"), sem("dkeep_ready"), sem("dlog_ready"), sem("dscale_ready"), sem("kvw_ready")
        gnb_ready, biasrow_psum, biasrow_ready = sem("gnb_ready"), sem("biasrow_psum"), sem("biasrow_ready")
        fsum_ready, fsum_spread, fq_ready, funscale_ready = sem("fsum_ready"), sem("fsum_spread"), sem("fq_ready"), sem("funscale_ready")
        ln_stats_done = [sem("ln1_stats_done"), sem("ln2_stats_done")]
        ln_mv_ready = [sem("ln1_mv_ready"), sem("ln2_mv_ready")]
        ln_step = [sem("ln1_step"), sem("ln2_step")]
        ln_coef_ready = [sem("ln1_coef_ready"), sem("ln2_coef_ready")]
        xn_ready = [sem("xn1_ready"), sem("xn2_ready")]
        turned = [sem("turned1"), sem("turned2")]
        xhi_ready = [sem("xhi1_ready"), sem("xhi2_ready")]
        xlo_ready = [sem("xlo1_ready"), sem("xlo2_ready")]
        k_ready, v_ready, r_ready = sem("k_ready"), sem("v_ready"), sem("r_ready")
        kcopy_ready, kw_ready, u_ready, scan_ready = sem("kcopy_ready"), sem("kw_ready"), sem("u_ready"), sem("scan_ready")
        gate_ready, o_ready = sem("gate_ready"), sem("o_ready")
        gn_stats_done, gn_mv_done, gn_sq_ready = sem("gn_stats_done"), sem("gn_mv_done"), sem("gn_sq_ready")
        gn_spread, gn_step, gn_var_ready, gn_coef_step, gn_coef_ready = sem("gn_spread"), sem("gn_step"), sem("gn_var_ready"), sem("gn_coef_step"), sem("gn_coef_ready")
        z_ready, zhi_ready, zlo_ready = sem("z_ready"), sem("zhi_ready"), sem("zlo_ready")
        y_ready, xb_ready, x2_ready = sem("y_ready"), sem("xb_ready"), sem("x2_ready")
        h_ready, relu_ready, hsq_ready, hhi_ready, hlo_ready = sem("h_ready"), sem("relu_ready"), sem("hsq_ready"), sem("hhi_ready"), sem("hlo_ready")
        hlo_last_ready = sem("hlo_last_ready")
        ffn_ready, ffn_sb_ready, out_ready = sem("ffn_ready"), sem("ffn_sb_ready"), sem("out_ready")

        block = ctx.enter_context(nc.Block())

        def need(eng, s, value):
            if not isinstance(value, int) or value > 0:
                eng.wait_ge(s, value)

        def live(b):
            return not isinstance(b, int) or 0 <= b < NB

        def rows(b, tile=0, tiles=CT):
            if isinstance(b, int):
                return x_all[:, b * N + tile * D:b * N + (tile + tiles) * D]
            return x_all[:, bass.ds(b * N + tile * D, tiles * D)]

        def run_slots(eng, slot):
            for i in range(LOOP[0]):
                slot(i)
            with eng.Fori(*LOOP) as i:
                slot(i)
            for i in range(LOOP[1], SLOTS):
                slot(i)

        @block.sync
        def _(sp):
            sp.dma_start(x_all[:, 0:N], x[:, 0:N]).then_inc(in_x[0], 16)
            sp.dma_start(w_raw[:, 0:3, :], w_qkv.rearrange("p (k n) -> p k n", k=3)).then_inc(in_wqkv, 16)
            sp.dma_start(x_all[:, N:2 * N], x[:, N:2 * N]).then_inc(in_x[1], 16)
            sp.dma_start(w_raw[:, 3, :], w_out).then_inc(in_wout, 16)
            sp.dma_start(x_all[:, 2 * N:NB * N], x[:, 2 * N:NB * N]).then_inc(in_x[2], 16)
            sp.dma_start(f_raw[:, 0, :], w_fc).then_inc(in_fc, 16)
            sp.dma_start(f_raw[:, 1, :], w_proj).then_inc(in_proj, 16)

            def slot(i):
                if live(i - 3):
                    need(sp, out_ready, i - 3 + 1)
                    b = i - 3
                    where = out[:, b * N:(b + 1) * N] if isinstance(b, int) else out[:, bass.ds(b * N, N)]
                    sp.dma_start(where, rows(b)).then_inc(stored, 16)

            run_slots(sp, slot)
            sp.wait_ge(stored, 16 * NB)

        @block.tensor
        def _(pe):
            def turn(n, b):
                pe.wait_ge(xn_ready[n], CT * (b + 1))
                for c in range(CD):
                    for t in range(CT):
                        last = nc.tensor.transpose(b_turn[:, c * T + t * P:c * T + (t + 1) * P],
                                                   xn[n][:, t * D + c * P:t * D + (c + 1) * P], ident[:])
                last.then_inc(turned[n], 1)

            def project(w, dst):
                for e in range(CD):
                    terms = [(wp, xp, c) for c in range(CD)
                             for wp, xp in ((w_hi, xt_hi[0]), (w_hi, xt_lo[0]), (w_lo, xt_hi[0]))]
                    for j, (wp, xp, c) in enumerate(terms):
                        last = nc.tensor.matmul(dst[:, e * T:(e + 1) * T], wp[:, w, c * D + e * P:c * D + (e + 1) * P],
                                                xp[:, c, :], start=(j == 0), stop=(j == len(terms) - 1))
                return last

            def projections(b):
                pe.wait_ge(xlo_ready[0], b + 1)
                if isinstance(b, int) and b == 0:
                    pe.wait_ge(wlo_ready, 1)
                need(pe, kcopy_ready, b)
                project(0, b_k).then_inc(k_ready, 1)
                if isinstance(b, int) and b == 0:
                    pe.wait_ge(wlo_ready, 2)
                need(pe, u_ready, b)
                project(1, b_v).then_inc(v_ready, 1)
                if isinstance(b, int) and b == 0:
                    pe.wait_ge(wlo_ready, 3)
                need(pe, gate_ready, b)
                project(2, b_r).then_inc(r_ready, 1)

            def spread_group_stats(b):
                pe.wait_ge(gn_sq_ready, b + 1)
                nc.tensor.matmul(b_turn[:, 0:1], mean_mat[:], gn_mv[:, 0:1], start=True, stop=True)
                nc.tensor.matmul(b_turn[:, 1:2], square_mat[:], gn_sq[:, 0:1], start=True,
                                 stop=True).then_inc(gn_spread, 1)

            def output_product(b):
                pe.wait_ge(zlo_ready, b + 1)
                need(pe, x2_ready, b)
                for t in range(CT):
                    terms = [(zp, wp, c) for c in range(CD)
                             for zp, wp in ((z_hi, w_hi), (z_hi, w_lo), (z_lo, w_hi))]
                    for j, (zp, wp, c) in enumerate(terms):
                        last = nc.tensor.matmul(b_y[:, t * D:(t + 1) * D], zp[:, c, t * P:(t + 1) * P],
                                                wp[:, 3, c * D:(c + 1) * D], start=(j == 0), stop=(j == len(terms) - 1))
                last.then_inc(y_ready, 1)

            def hidden_product(b):
                pe.wait_ge(xlo_ready[1], b + 1)
                for p, (h0, h1) in enumerate(PAIRS):
                    if p == 0:
                        need(pe, relu_ready, 3 * b)
                    elif p == 1:
                        need(pe, relu_ready, 3 * b - 1)
                    else:
                        need(pe, relu_ready, 3 * b + 1)
                    for h in range(h0, h1):
                        terms = [(xp, c) for c in range(CD) for xp in (xt_hi[1], xt_lo[1])]
                        for j, (xp, c) in enumerate(terms):
                            last = nc.tensor.matmul(b_h[p][:, (h - h0) * T:(h - h0 + 1) * T],
                                                    f_q[:, 0, c * H + h * P:c * H + (h + 1) * P], xp[:, c, :],
                                                    start=(j == 0), stop=(j == len(terms) - 1))
                    last.then_inc(h_ready, 1)

            def last_product(b):
                pe.wait_ge(hlo_ready, 2 * (b + 1))
                pe.wait_ge(hlo_last_ready, b + 1)
                need(pe, ffn_sb_ready, b)
                for t in range(CT):
                    terms = [(hp, h) for h in range(CH) for hp in (h_hi, h_lo)]
                    for j, (hp, h) in enumerate(terms):
                        last = nc.tensor.matmul(b_o[:, t * D:(t + 1) * D], hp[:, h * T + t * P:h * T + (t + 1) * P],
                                                f_q[:, 1, h * D:(h + 1) * D], start=(j == 0), stop=(j == len(terms) - 1))
                last.then_inc(ffn_ready, 1)

            def spread_weight_max(step, first, count):
                pe.wait_ge(wmax_ready, step)
                nc.tensor.transpose(b_o[0:count, 0:P], w_max[:, first:first + count], ident[:]).then_inc(wmax_turned, 1)
                pe.wait_ge(wdiag_ready, step)
                nc.tensor.matmul(b_o[:, P:P + count], ones[0:count, :], w_max_diag[0:count, first:first + count],
                                 start=True, stop=True).then_inc(wmax_spread, 1)

            def bias_product():
                pe.wait_ge(gnb_ready, 1)
                pe.wait_ge(in_wout, 16)
                for c in range(CD):
                    last = nc.tensor.matmul(b_h[0][:, 0:D], gnb_wide[:, c, :], w_raw[:, 3, c * D:(c + 1) * D],
                                            start=(c == 0), stop=(c == CD - 1))
                last.then_inc(biasrow_psum, 1)

            def spread_ffn_sums():
                pe.wait_ge(fsum_ready, 2)
                nc.tensor.matmul(b_o[:, 256:258], ones[:], f_sum[:], start=True, stop=True).then_inc(fsum_spread, 1)

            def slot(i):
                head = isinstance(i, int) and i < 2
                if live(i):
                    projections(i)
                if head and i == 1:
                    spread_weight_max(2, 3, 1)
                    bias_product()
                    spread_group_stats(0)
                if live(i + 1):
                    if isinstance(i, int) and i == 0:
                        pe.wait_ge(xlo_ready[0], 1)
                    elif isinstance(i, int) and i == 1:
                        pe.wait_ge(gn_step, 1)
                    else:
                        need(pe, xlo_ready[1], i - 2 + 1)
                    turn(0, i + 1)
                drain = isinstance(i, int) and i >= NB
                if live(i - 1) and not drain:
                    output_product(i - 1)
                if head and i == 1:
                    spread_ffn_sums()
                if live(i - 3):
                    last_product(i - 3)
                if live(i - 2):
                    if isinstance(i, int) and i == 2:
                        pe.wait_ge(fq_ready, 1)
                        pe.wait_ge(biasrow_ready, 1)
                    hidden_product(i - 2)
                if live(i - 1) and drain:
                    output_product(i - 1)
                if live(i) and not (isinstance(i, int) and i == 0):
                    if not isinstance(i, int) or i + 1 < NB:
                        pe.wait_ge(xlo_ready[0], i + 2)
                    else:
                        pe.wait_ge(xlo_ready[1], i - 2 + 1)
                    spread_group_stats(i)
                if live(i - 1):
                    if isinstance(i, int) and i >= NB:
                        pe.wait_ge(gn_step, NB)
                    else:
                        pe.wait_ge(gn_step, i + 1)
                    turn(1, i - 1)

            pe.wait_ge(consts_ready, 1)
            turn(0, 0)
            spread_weight_max(1, 0, 3)
            run_slots(pe, slot)

        @block.vector
        def _(dve):
            def need_apart(s, value):
                need(dve, s, value)
                if not isinstance(value, int):
                    nc.vector.memset(wait_taker[:], 0.0)

            steps = [0]

            def step(ins):
                steps[0] += 1
                ins.then_inc(setup_step, 1)
                dve.wait_ge(setup_step, steps[0])

            def layer_stats(n, b):
                for t in range(CT):
                    last = nc.vector.bn_stats(ln_stats[n][:, t, :], rows(b, t, 1))
                last.then_inc(ln_stats_done[n], 1)
                need(dve, ln_coef_ready[n], b)
                need_apart(ln_stats_done[n], b + 1)
                for t in range(CT):
                    last = nc.vector.bn_aggr(ln_mv[n][:, t, :], ln_stats[n][:, t, :])
                last.then_inc(ln_mv_ready[n], 1)

            def first_stats(b):
                if isinstance(b, int) and b < 3:
                    dve.wait_ge(in_x[b], 16)
                layer_stats(0, b)

            def low_part(n, b):
                dve.wait_ge(xhi_ready[n], b + 1)
                nc.vector.tensor_tensor(xt_lo[n][:].rearrange("p c t -> p (c t)"), b_turn[:],
                                        xt_hi[n][:].rearrange("p c t -> p (c t)"), ALU.subtract).then_inc(xlo_ready[n], 1)

            def kv(b):
                dve.wait_ge(v_ready, b + 1)
                dve.wait_ge(kw_ready, b + 1)
                nc.vector.tensor_tensor(u_sb[:].rearrange("p c t -> p (c t)"), b_v[:], kw_sb[:], ALU.mult).then_inc(u_ready, 1)

            def scan(b):
                dve.wait_ge(u_ready, b + 1)
                need(dve, o_ready, b)
                for c in range(CD):
                    last = nc.vector.tensor_tensor_scan(state[:, c, :], d_keep[:, c:c + 1].to_broadcast([P, T]),
                                                        u_sb[:, c, :], 0.0, ALU.mult, ALU.add)
                last.then_inc(scan_ready, 1)

            def group_stats(b):
                dve.wait_ge(o_ready, b + 1)
                nc.vector.bn_stats(gn_stats[:], o_sb[:]).then_inc(gn_stats_done, 1)
                need(dve, gn_spread, b)
                need_apart(gn_stats_done, b + 1)
                nc.vector.bn_aggr(gn_mv[:], gn_stats[:]).then_inc(gn_mv_done, 1)
                dve.wait_ge(gn_mv_done, b + 1)
                nc.vector.scalar_tensor_tensor(out=gn_sq[:], in0=gn_mv[:, 0:1], scalar=gn_mv[:, 0:1], in1=gn_mv[:, 1:2],
                                               op0=ALU.mult, op1=ALU.add).then_inc(gn_sq_ready, 1)

            def group_variance(b):
                dve.wait_ge(gn_spread, b + 1)
                need(dve, gn_coef_ready, b)
                nc.vector.tensor_copy(gn_all[:], b_turn[:, 0:2]).then_inc(gn_step, 1)
                dve.wait_ge(gn_step, b + 1)
                nc.vector.scalar_tensor_tensor(out=gn_nvar[:], in0=gn_all[:, 0:1], scalar=gn_all[:, 0:1],
                                               in1=gn_all[:, 1:2], op0=ALU.mult, op1=ALU.subtract).then_inc(gn_var_ready, 1)
                dve.wait_ge(gn_var_ready, 2 * b + 1)
                nc.vector.tensor_scalar(gn_nveps[:], gn_nvar[:], 0.0, EPS / Z_SCALE ** 2, ALU.min,
                                        ALU.subtract).then_inc(gn_var_ready, 1)

            def z_low(b):
                dve.wait_ge(zhi_ready, b + 1)
                nc.vector.tensor_tensor(z_lo[:].rearrange("p c t -> p (c t)"), z_sb[:],
                                        z_hi[:].rearrange("p c t -> p (c t)"), ALU.subtract).then_inc(zlo_ready, 1)

            def add_attention(b):
                dve.wait_ge(y_ready, b + 1)
                dve.wait_ge(xb_ready, b + 1)
                nc.vector.scalar_tensor_tensor(out=rows(b), in0=b_y[:], scalar=y_unscale[:], in1=rows(b),
                                               op0=ALU.mult, op1=ALU.add).then_inc(x2_ready, 1)
                need_apart(x2_ready, b + 1)
                layer_stats(1, b)

            def squares(b, part):
                c0, c1, c2 = ((0, 2, 2), (2, 4, CH))[part]
                dve.wait_ge(relu_ready, 3 * b + (1, 3)[part])
                if part:
                    need(dve, hlo_last_ready, b)
                nc.vector.tensor_tensor(h_sq[:, c0 * T:c2 * T], h_relu[:, c0 * T:c2 * T], h_relu[:, c0 * T:c2 * T],
                                        ALU.mult).then_inc(hsq_ready, 1)
                dve.wait_ge(hsq_ready, 2 * b + part + 1)
                dve.wait_ge(hhi_ready, 2 * b + part + 1)
                nc.vector.tensor_tensor(h_lo[:, c0 * T:c1 * T], h_sq[:, c0 * T:c1 * T], h_hi[:, c0 * T:c1 * T],
                                        ALU.subtract).then_inc(hlo_ready, 1)

            def weight_max(w0, w1, src):
                nc.vector.tensor_reduce(w_max[:, w0:w1], src, AX.X, ALU.max, apply_absolute_value=True).then_inc(wmax_ready, 1)

            def weight_scale(n, w0, w1):
                count = w1 - w0
                dve.wait_ge(wmax_turned, n)
                step(nc.vector.tensor_reduce(w_max_all[0:count, n - 1:n], b_o[0:count, 0:P], AX.X, ALU.max))
                step(nc.vector.tensor_scalar(w_max_all[0:count, n - 1:n], w_max_all[0:count, n - 1:n], 1e-30, None, ALU.max))
                nc.vector.tensor_scalar(w_max_diag[0:count, w0:w1], ident[0:count, 0:count],
                                        w_max_all[0:count, n - 1:n], None, ALU.mult).then_inc(wdiag_ready, 1)
                dve.wait_ge(wmax_spread, n)
                step(nc.vector.tensor_copy(w_pow[:, w0:w1], b_o[:, P:P + count]))
                step(nc.vector.tensor_scalar(w_pow[:, w0:w1].bitcast(U32), w_pow[:, w0:w1].bitcast(U32), EXPONENT, None,
                                             ALU.bitwise_and))
                step(nc.vector.reciprocal(w_inv[:, w0:w1], w_pow[:, w0:w1]))
                nc.vector.tensor_scalar(w_mul[:, w0:w1], w_inv[:, w0:w1], W_SCALE, None, ALU.mult).then_inc(wscale_ready, 1)
                step(nc.vector.tensor_scalar(unscale[:, w0:w1], w_pow[:, w0:w1], 1.0 / (W_SCALE * X_SCALE), None, ALU.mult))

            def weight_low(w, src):
                dve.wait_ge(whi_ready, w + 1)
                nc.vector.scalar_tensor_tensor(out=w_lo[:, w, :], in0=src, scalar=w_mul[:, w:w + 1],
                                               in1=w_hi[:, w, :], op0=ALU.mult, op1=ALU.subtract).then_inc(wlo_ready, 1)

            def ternary():
                dve.wait_ge(fsum_spread, 1)
                step(nc.vector.tensor_scalar(f_mean[:], b_o[:, 256:258], 1.0 / (D * H), 1e-5, ALU.mult, ALU.max))
                step(nc.vector.tensor_scalar(f_thr[:], f_mean[:], 0.7, None, ALU.mult))
                step(nc.vector.tensor_scalar(f_nthr[:], f_thr[:], -1.0, None, ALU.mult))
                for w in range(2):
                    step(nc.vector.tensor_scalar(f_neg[:, w, :], f_raw[:, w, :], f_nthr[:, w:w + 1], None, ALU.is_lt))
                    nc.vector.scalar_tensor_tensor(out=f_q[:, w, :], in0=f_raw[:, w, :], scalar=f_thr[:, w:w + 1],
                                                   in1=f_neg[:, w, :], op0=ALU.is_gt, op1=ALU.subtract).then_inc(fq_ready, 1)
                step(nc.vector.tensor_tensor(f_m2[:], f_mean[:, 0:1], f_mean[:, 0:1], ALU.mult))
                nc.vector.tensor_scalar(f_unscale[:], f_m2[:], f_mean[:, 1:2], 1.0 / H_SCALE ** 2, ALU.mult,
                                        ALU.mult).then_inc(funscale_ready, 1)

            dve.wait_ge(dexp_ready, 1)
            step(nc.vector.tensor_scalar(d_exp1[:], d_exp[:], 1.0, None, ALU.add))
            step(nc.vector.reciprocal(d_sig[:], d_exp1[:]))
            nc.vector.tensor_scalar(d_keep[:], d_sig[:], 1e-7, None, ALU.max).then_inc(dkeep_ready, 1)
            first_stats(0)
            dve.wait_ge(in_wqkv, 16)
            weight_max(0, 3, w_raw[:, 0:3, :])
            dve.wait_ge(consts_ready, 1)
            weight_scale(1, 0, 3)
            low_part(0, 0)
            for w in range(3):
                weight_low(w, w_raw[:, w, :])
            dve.wait_ge(dscale_ready, 1)
            step(nc.vector.tensor_scalar(d_ratio[:], d_scale[:].rearrange("p c t -> p (c t)"), 1e10, 1.0, ALU.mult, ALU.min))
            nc.vector.tensor_scalar(kv_weight[:], d_ratio[:], unscale[:, 1:2], None, ALU.mult).then_inc(kvw_ready, 1)

            def slot(i):
                first = isinstance(i, int) and i == 0
                second = isinstance(i, int) and i == 1
                if live(i + 1):
                    first_stats(i + 1)
                if live(i - 1) and not second:
                    z_low(i - 1)
                if live(i - 3):
                    squares(i - 3, 1)
                if live(i - 2):
                    low_part(1, i - 2)
                if live(i):
                    kv(i)
                    scan(i)
                if second:
                    weight_scale(2, 3, 4)
                    step(nc.vector.tensor_scalar(y_unscale[:], unscale[:, 3:4], X_SCALE / Z_SCALE, None, ALU.mult))
                    weight_low(3, wo_gn[:])
                    group_variance(0)
                    z_low(0)
                if live(i + 1):
                    low_part(0, i + 1)
                if first:
                    dve.wait_ge(in_wout, 16)
                    for c in range(CD):
                        last = nc.vector.tensor_scalar(wo_gn[:, c * D:(c + 1) * D], w_raw[:, 3, c * D:(c + 1) * D],
                                                       gn_w_c[:, c:c + 1], None, ALU.mult)
                    step(last)
                    weight_max(3, 4, wo_gn[:])
                if live(i - 1):
                    add_attention(i - 1)
                if live(i):
                    group_stats(i)
                if live(i) and not first:
                    group_variance(i)
                if second:
                    ternary()
                if live(i - 2):
                    squares(i - 2, 0)

            run_slots(dve, slot)

        @block.scalar
        def _(act):
            def normalise(n, b):
                act.wait_ge(ln_coef_ready[n], b + 1)
                need(act, turned[n], b)
                for t in range(CT):
                    nc.scalar.activation(xn[n][:, t * D:(t + 1) * D], rows(b, t, 1), ACT.Identity,
                                         bias=ln_bias[n][:, t:t + 1], scale=ln_rs[n][:, t:t + 1]).then_inc(xn_ready[n], 1)

            def high_part(n, b):
                act.wait_ge(turned[n], b + 1)
                if n == 0:
                    need(act, r_ready, b)
                else:
                    need(act, h_ready, 3 * b)
                nc.scalar.activation(xt_hi[n][:].rearrange("p c t -> p (c t)"), b_turn[:], ACT.Copy).then_inc(xhi_ready[n], 1)

            def copy_k(b):
                act.wait_ge(k_ready, b + 1)
                need(act, kw_ready, b)
                nc.scalar.activation(k_sb[:], b_k[:], ACT.Copy, scale=unscale[:, 0:1]).then_inc(kcopy_ready, 1)

            def gate_of(b):
                act.wait_ge(r_ready, b + 1)
                need(act, o_ready, b)
                nc.scalar.activation(gate[:], b_r[:], ACT.Sigmoid, scale=unscale[:, 2:3]).then_inc(gate_ready, 1)

            def group_normalise(b):
                act.wait_ge(gn_coef_ready, b + 1)
                need(act, zlo_ready, b)
                nc.scalar.activation(z_sb[:], o_sb[:], ACT.Identity, bias=gn_bias[:], scale=gn_rs[:]).then_inc(z_ready, 1)
                act.wait_ge(z_ready, b + 1)
                need(act, y_ready, b)
                nc.scalar.activation(z_hi[:].rearrange("p c t -> p (c t)"), z_sb[:], ACT.Copy).then_inc(zhi_ready, 1)

            def relu(b, p):
                h0, h1 = PAIRS[p]
                act.wait_ge(h_ready, 3 * b + p + 1)
                need(act, hsq_ready, 2 * b)
                nc.scalar.activation(h_relu[:, h0 * T:h1 * T], b_h[p][:, 0:(h1 - h0) * T], ACT.Relu,
                                     scale=H_SCALE / X_SCALE).then_inc(relu_ready, 1)

            def square_high(b, part):
                c0, c1 = ((0, 2), (2, CH))[part]
                act.wait_ge(relu_ready, 3 * b + (1, 3)[part])
                need(act, ffn_ready, b)
                nc.scalar.activation(h_hi[:, c0 * T:c1 * T], h_relu[:, c0 * T:c1 * T], ACT.Square).then_inc(hhi_ready, 1)

            def copy_ffn(b):
                act.wait_ge(ffn_ready, b + 1)
                need(act, out_ready, b)
                nc.scalar.activation(ffn_out[:], b_o[:], ACT.Copy, scale=f_unscale[:]).then_inc(ffn_sb_ready, 1)

            def weight_high(w, src):
                nc.scalar.activation(w_hi[:, w, :], src, ACT.Copy, scale=w_mul[:, w:w + 1]).then_inc(whi_ready, 1)

            act.dma_start(cols[:], columns).then_inc(in_cols, 16)
            act.wait_ge(in_cols, 16)
            nc.scalar.activation(d_exp[:], decay_c, ACT.Exp, scale=-1.0).then_inc(dexp_ready, 1)
            act.wait_ge(dkeep_ready, 1)
            nc.scalar.activation(d_log[:], d_keep[:], ACT.Ln).then_inc(dlog_ready, 1)
            act.wait_ge(dlog_ready, 1)
            act.wait_ge(consts_ready, 1)
            for c in range(CD):
                last = nc.scalar.activation(d_scale[:, c, :], position[:], ACT.Exp, scale=d_log[:, c:c + 1])
            last.then_inc(dscale_ready, 1)
            normalise(0, 0)
            high_part(0, 0)
            act.wait_ge(wscale_ready, 1)
            for w in range(3):
                weight_high(w, w_raw[:, w, :])

            def slot(i):
                second = isinstance(i, int) and i == 1
                if live(i - 1) and not second:
                    group_normalise(i - 1)
                if live(i):
                    copy_k(i)
                if live(i - 3):
                    square_high(i - 3, 1)
                if live(i - 2):
                    high_part(1, i - 2)
                if live(i + 1):
                    normalise(0, i + 1)
                if live(i):
                    gate_of(i)
                if second:
                    act.wait_ge(wscale_ready, 2)
                    weight_high(3, wo_gn[:])
                    act.wait_ge(biasrow_psum, 1)
                    nc.scalar.activation(bias_row[:], b_h[0][:, 0:D], ACT.Copy).then_inc(biasrow_ready, 1)
                    group_normalise(0)
                if live(i + 1):
                    high_part(0, i + 1)
                if second:
                    for w, arrived in enumerate((in_fc, in_proj)):
                        act.wait_ge(arrived, 16)
                        if w:
                            act.wait_ge(fsum_ready, 1)
                        nc.scalar.activation(f_abs[:], f_raw[:, w, :], ACT.Abs, accum_out=f_sum[:, w:w + 1]).then_inc(fsum_ready, 1)
                if live(i - 3):
                    if isinstance(i, int) and i == 3:
                        act.wait_ge(funscale_ready, 1)
                    copy_ffn(i - 3)
                if live(i - 2):
                    relu(i - 2, 0)
                    square_high(i - 2, 0)
                if live(i - 1):
                    normalise(1, i - 1)
                if live(i - 2):
                    relu(i - 2, 1)
                    relu(i - 2, 2)

            run_slots(act, slot)

        @block.gpsimd
        def _(pool):
            def layer_coefficients(n, b):
                need(pool, xn_ready[n], CT * b)
                pool.wait_ge(ln_mv_ready[n], b + 1)
                nc.gpsimd.tensor_tensor(ln_nm[n][:], ln_mv[n][:, :, 0], minus_one[:], ALU.mult).then_inc(ln_step[n], 1)
                nc.gpsimd.tensor_scalar(ln_var[n][:], ln_mv[n][:, :, 1], X_SCALE ** -2, EPS * X_SCALE ** -2,
                                        ALU.mult, ALU.add).then_inc(ln_step[n], 1)
                pool.wait_ge(ln_step[n], 3 * b + 2)
                nc.gpsimd.tensor_tensor(ln_rs[n][:], ln_var[n][:], minus_half[:], ALU.pow).then_inc(ln_step[n], 1)
                pool.wait_ge(ln_step[n], 3 * b + 3)
                nc.gpsimd.tensor_tensor(ln_bias[n][:], ln_nm[n][:], ln_rs[n][:], ALU.mult).then_inc(ln_coef_ready[n], 1)

            def group_coefficients(b):
                need(pool, z_ready, b)
                pool.wait_ge(gn_var_ready, 2 * b + 2)
                nc.gpsimd.tensor_tensor(gn_veps[:], gn_nveps[:], minus_one[:, 0:1], ALU.mult).then_inc(gn_coef_step, 1)
                nc.gpsimd.tensor_scalar(gn_nm[:], gn_all[:, 0:1], -Z_SCALE, 0.0, ALU.mult, ALU.add).then_inc(gn_coef_step, 1)
                pool.wait_ge(gn_coef_step, 3 * b + 2)
                nc.gpsimd.tensor_tensor(gn_rs[:], gn_veps[:], minus_half[:, 0:1], ALU.pow).then_inc(gn_coef_step, 1)
                pool.wait_ge(gn_coef_step, 3 * b + 3)
                nc.gpsimd.tensor_tensor(gn_bias[:], gn_nm[:], gn_rs[:], ALU.mult).then_inc(gn_coef_ready, 1)

            def weigh_k(b):
                pool.wait_ge(kcopy_ready, b + 1)
                need(pool, u_ready, b)
                nc.gpsimd.tensor_tensor(kw_sb[:], k_sb[:], kv_weight[:], ALU.mult).then_inc(kw_ready, 1)

            def gate_state(b):
                pool.wait_ge(gate_ready, b + 1)
                pool.wait_ge(scan_ready, b + 1)
                need(pool, z_ready, b)
                nc.gpsimd.tensor_tensor(o_sb[:], gate[:], state[:].rearrange("p c t -> p (c t)"), ALU.mult).then_inc(o_ready, 1)

            def add_bias(b):
                pool.wait_ge(xn_ready[0], CT * (b + 1))
                tiled = rows(b).rearrange("p (t d) -> p t d", t=CT)
                nc.gpsimd.tensor_tensor(tiled, tiled, bias_row[:].rearrange("p (o d) -> p o d", o=1).to_broadcast([P, CT, D]),
                                        ALU.add).then_inc(xb_ready, 1)

            def last_low(b):
                pool.wait_ge(hsq_ready, 2 * b + 2)
                pool.wait_ge(hhi_ready, 2 * b + 2)
                nc.gpsimd.tensor_tensor(h_lo[:, 4 * T:], h_sq[:, 4 * T:], h_hi[:, 4 * T:], ALU.subtract).then_inc(hlo_last_ready, 1)

            def add_ffn(b):
                pool.wait_ge(ffn_sb_ready, b + 1)
                nc.gpsimd.tensor_tensor(rows(b), rows(b), ffn_out[:], ALU.add).then_inc(out_ready, 1)

            nc.gpsimd.memset(ident[:], 0.0).then_inc(consts_step, 1)
            pool.wait_ge(consts_step, 1)
            nc.gpsimd.affine_select(out=ident[:], in_=ident[:], compare_op=ALU.not_equal, fill=1.0, base=0,
                                    pattern=[[-1, P]], channel_multiplier=1)
            nc.gpsimd.memset(minus_half[:], -0.5)
            nc.gpsimd.memset(minus_one[:], -1.0)
            nc.gpsimd.memset(ones[:], 1.0)
            nc.gpsimd.memset(mean_mat[:], 1.0 / (P * Z_SCALE))
            nc.gpsimd.memset(square_mat[:], 1.0 / (P * Z_SCALE ** 2))
            nc.gpsimd.iota(position[:], pattern=[[1, T]], base=0, channel_multiplier=0,
                           allow_small_or_imprecise_dtypes=True).then_inc(consts_ready, 1)
            pool.wait_ge(consts_ready, 1)
            layer_coefficients(0, 0)
            pool.wait_ge(in_cols, 16)
            for c in range(CD):
                last = nc.gpsimd.tensor_scalar(gnb_wide[:, c, :], ones[:], gn_b_c[:, c:c + 1], 0.0, ALU.mult, ALU.add)
            last.then_inc(gnb_ready, 1)
            pool.wait_ge(kvw_ready, 1)

            def slot(i):
                second = isinstance(i, int) and i == 1
                if live(i + 1):
                    layer_coefficients(0, i + 1)
                if live(i - 3):
                    last_low(i - 3)
                if live(i):
                    weigh_k(i)
                    if second:
                        group_coefficients(0)
                    gate_state(i)
                if second:
                    pool.wait_ge(biasrow_ready, 1)
                    add_bias(0)
                if live(i) and not (isinstance(i, int) and i == 0):
                    add_bias(i)
                if live(i - 1):
                    layer_coefficients(1, i - 1)
                if live(i) and not (isinstance(i, int) and i == 0):
                    group_coefficients(i)
                if live(i - 3):
                    add_ffn(i - 3)

            run_slots(pool, slot)


def kernel(L0_attn_x, L0_attn_Wr, L0_attn_Wk, L0_attn_Wv, L0_attn_Wo, L0_attn_decay, L0_attn_gn_weight,
           L0_attn_gn_bias, L0_ffn_w_fc, L0_ffn_w_proj):
    import concourse.bacc as bacc
    from concourse.bass_utils import run_bass_kernel_spmd

    def by_partition(a):
        a = np.asarray(a)
        a = a.reshape(a.shape[0] // P, P, -1)
        return np.ascontiguousarray(a.transpose(1, 0, 2).reshape(P, -1))

    B, T, D = L0_attn_x.shape
    arrays = {
        "in_x": by_partition(np.asarray(L0_attn_x).reshape(B * T, D)),
        "in_w_qkv": np.ascontiguousarray(np.concatenate([by_partition(np.asarray(w).T) for w in (L0_attn_Wk, L0_attn_Wv, L0_attn_Wr)], axis=1)),
        "in_w_out": by_partition(np.asarray(L0_attn_Wo).T),
        "in_columns": np.ascontiguousarray(np.concatenate(
            [by_partition(np.asarray(a).reshape(-1, 1)) for a in (L0_attn_decay, L0_attn_gn_weight, L0_attn_gn_bias)], axis=1)),
        "in_w_fc": by_partition(np.asarray(L0_ffn_w_fc).T),
        "in_w_proj": by_partition(np.asarray(L0_ffn_w_proj).T),
    }
    nc = bacc.Bacc("TRN2", target_bir_lowering=False, num_devices=1)
    args = [nc.dram_tensor(n, a.shape, mybir.dt.from_np(a.dtype), kind="ExternalInput").ap() for n, a in arrays.items()]
    result = nc.dram_tensor("result", arrays["in_x"].shape, mybir.dt.float32, kind="ExternalOutput").ap()
    decay_block_kernel(nc, *args, result)
    r = run_bass_kernel_spmd(nc, [arrays], core_ids=[0])
    got = r.results[0]["result"].reshape(P, B * T // P, D)
    return np.ascontiguousarray(got.transpose(1, 0, 2)).reshape(B, T, D)
```

```python
import numpy as np
import concourse.bass as bass
from concourse import mybir
from contextlib import ExitStack

P = 128


def decay_block_kernel(nc, x, w_qkv, w_out, columns, w_fc, w_proj, out):
    F32, F16, U32 = mybir.dt.float32, mybir.dt.float16, mybir.dt.uint32
    ALU, ACT, AX = mybir.AluOpType, mybir.ActivationFunctionType, mybir.AxisListType

    D = 256
    NB = 8
    T = x.shape[1] // NB // D * P
    CD, CT = D // P, T // P
    N = CT * D
    H = w_fc.shape[1] // CD
    CH = H // P
    assert T == D and N == 512
    EPS = 1e-5
    EXPONENT = 0x7F800000

    X_SCALE = 2.0 ** 8
    Z_MAX = float(np.sqrt(T * D))
    W_SCALE = 2.0 ** 14
    H_SCALE = 2.0 ** -1
    WARM_UP = (9, 1, 4)
    ATTENTION_LOOP = (3, NB - 2)
    FFN_LOOP = (2, NB - 2)

    PAIRS = [(0, 2), (2, 4), (4, CH)]

    ctx = ExitStack()
    with ctx:
        def sb(name, shape, dt):
            return ctx.enter_context(nc.sbuf_tensor(name, shape, dt))

        def sem(name):
            return ctx.enter_context(nc.semaphore(name))

        ident = sb("ident", [P, P], F32)
        ones = sb("ones", [P, P], F32)
        mean_mat = sb("mean_mat", [P, P], F32)
        minus_half = sb("minus_half", [P, CT], F32)
        minus_one = sb("minus_one", [P, CT], F32)
        zeros = sb("zeros", [P, T], F32)
        cols = sb("cols", [P, 3 * CD], F32)
        decay_c, gn_w_c, gn_b_c = cols[:, 0:CD], cols[:, CD:2 * CD], cols[:, 2 * CD:3 * CD]
        w_raw = sb("w_raw", [P, 4, CD * D], F32)
        w_hi = sb("w_hi", [P, 4, CD * D], F16)
        w_lo = sb("w_lo", [P, 4, CD * D], F16)
        wr_scaled = sb("wr_scaled", [P, CD * D], F32)
        w_max = sb("w_max", [P, 5], F32)
        w_max_all = sb("w_max_all", [4, 2], F32)
        w_max_diag = sb("w_max_diag", [4, 8], F32)
        w_pow = sb("w_pow", [P, 5], F32)
        w_inv = sb("w_inv", [P, 5], F32)
        w_mul = sb("w_mul", [P, 5], F32)
        unscale = sb("unscale", [P, 5], F32)
        gn_w_max = sb("gn_w_max", [P, 1], F32)
        gn_b_max = sb("gn_b_max", [P, 1], F32)
        gn_wz = sb("gn_wz", [P, CD], F32)
        gn_bz = sb("gn_bz", [P, CD], F32)
        y_unscale = sb("y_unscale", [P, 1], F32)
        d_sig = sb("d_sig", [P, CD], F32)
        d_keep = sb("d_keep", [P, CD], F32)
        d_power = sb("d_power", [P, CD, T], F32)
        kv_weight = sb("kv_weight", [P, CD * T], F32)
        f_raw = sb("f_raw", [P, 2, CD * H], F32)
        f_abs = sb("f_abs", [P, CD * H], F32)
        f_sum = sb("f_sum", [P, 2], F32)
        f_mean = sb("f_mean", [P, 2], F32)
        f_thr = sb("f_thr", [P, 2], F32)
        f_nthr = sb("f_nthr", [P, 2], F32)
        f_neg = sb("f_neg", [P, 2, CD * H], F16)
        f_q = sb("f_q", [P, 2, CD * H], F16)
        f_m2 = sb("f_m2", [P, 1], F32)
        f_unscale = sb("f_unscale", [P, 1], F32)

        x_all = sb("x_all", [P, NB * N], F32)
        ln_stats = [sb(f"ln{n}_stats", [P, CT, 6], F32) for n in (1, 2)]
        ln_mv = [sb(f"ln{n}_mv", [P, CT, 2], F32) for n in (1, 2)]
        ln_var = [sb(f"ln{n}_var", [P, CT], F32) for n in (1, 2)]
        ln_nm = [sb(f"ln{n}_nm", [P, CT], F32) for n in (1, 2)]
        ln_rs = [sb(f"ln{n}_rs", [P, CT], F32) for n in (1, 2)]
        ln_bias = [sb(f"ln{n}_bias", [P, CT], F32) for n in (1, 2)]
        xn = [sb(f"xn{n}", [P, N], F32) for n in (1, 2)]
        xt_hi = [sb(f"xt{n}_hi", [P, NB * CD * T], F16) for n in (1, 2)]
        xt_lo = [sb(f"xt{n}_lo", [P, NB * CD * T], F16) for n in (1, 2)]
        kw_sb = sb("kw_sb", [P, N], F32)
        u_sb = sb("u_sb", [P, CD, T], F32)
        state = sb("state", [P, CD, T], F32)
        gate = sb("gate", [P, N], F32)
        o_all = sb("o_all", [P, NB * N], F32)
        gn_sums = sb("gn_sums", [P, 2], F32)
        gn_copies = [sb(f"gn_{what}", [P, N], F32) for what in ("same", "squared")]
        gn_all = sb("gn_all", [P, 2], F32)
        gn_nvar = sb("gn_nvar", [P, 1], F32)
        gn_nveps = sb("gn_nveps", [P, 1], F32)
        gn_veps = sb("gn_veps", [P, 1], F32)
        gn_rs = sb("gn_rs", [P, 1], F32)
        gn_scale = sb("gn_scale", [P, CD], F32)
        gn_shift = sb("gn_shift", [P, CD], F32)
        gn_bias = sb("gn_bias", [P, CD], F32)
        z_sb = sb("z_sb", [P, N], F32)
        z_hi = sb("z_hi", [P, NB * CD * T], F16)
        z_lo = sb("z_lo", [P, NB * CD * T], F16)
        h_relu = sb("h_relu", [P, CH * T], F32)
        h_sq = sb("h_sq", [P, CH * T], F32)
        h_hi = [sb(f"h_hi{n}", [P, CH * T], F16) for n in range(2)]
        h_lo = [sb(f"h_lo{n}", [P, CH * T], F16) for n in range(2)]
        ffn_out = sb("ffn_out", [P, N], F32)

        bank = [ctx.enter_context(nc.psum_tensor(f"bank_{n}", [P, 512], F32))
                for n in ("turn", "k", "v", "r", "y", "o", "h0", "h1")]
        b_turn, b_k, b_v, b_r, b_y, b_o = bank[:6]
        b_h = [bank[6], bank[7], b_k]
        last_banks = [b_turn[:, 0:D], b_y[:, 0:D]]
        y_bank = lambda b: {NB - 2: b_v, NB - 1: b_r}.get(b, b_y) if isinstance(b, int) else b_y

        in_x = [sem("in_x0"), sem("in_x1"), sem("in_x2"), sem("in_x_rest")]
        in_wqkv = [sem("in_wk"), sem("in_wv"), sem("in_wr")]
        in_wout, in_cols = sem("in_wout"), sem("in_cols")
        in_fc, in_proj, stored = sem("in_fc"), sem("in_proj"), sem("stored")
        consts_step, consts_ready = sem("consts_step"), sem("consts_ready")
        setup_step = sem("setup_step")
        wmax_ready, wmax_turned, wdiag_ready, wmax_spread = sem("wmax_ready"), sem("wmax_turned"), sem("wdiag_ready"), sem("wmax_spread")
        wscale_ready, unscale_ready, whi_ready, wlo_ready = sem("wscale_ready"), sem("unscale_ready"), sem("whi_ready"), sem("wlo_ready")
        wr_scaled_ready, wlo_r_ready = sem("wr_scaled_ready"), sem("wlo_r_ready")
        dsig_ready, dkeep_ready, dpower_ready, kvweight_ready = sem("dsig_ready"), sem("dkeep_ready"), sem("dpower_ready"), sem("kvweight_ready")
        gnaffine_ready = sem("gnaffine_ready")
        fsum_ready, fsum_spread, fthr_ready, funscale_ready = sem("fsum_ready"), sem("fsum_spread"), sem("fthr_ready"), sem("funscale_ready")
        fq_ready = [sem("fq_fc_ready"), sem("fq_proj_ready")]
        fneg_ready = [sem("fneg_fc_ready"), sem("fneg_proj_ready")]
        ln_stats_done = [sem("ln1_stats_done"), sem("ln2_stats_done")]
        ln_mv_ready = [sem("ln1_mv_ready"), sem("ln2_mv_ready")]
        ln_step = [sem("ln1_step"), sem("ln2_step")]
        ln_coef_ready = [sem("ln1_coef_ready"), sem("ln2_coef_ready")]
        xn_ready = [sem("xn1_ready"), sem("xn2_ready")]
        turned = [sem("turned1"), sem("turned2")]
        xhi_ready = [sem("xhi1_ready"), sem("xhi2_ready")]
        xlo_ready = [sem("xlo1_ready"), sem("xlo2_ready")]
        k_ready, v_ready, r_ready = sem("k_ready"), sem("v_ready"), sem("r_ready")
        kw_ready, u_ready, scan_ready = sem("kw_ready"), sem("u_ready"), sem("scan_ready")
        gate_ready, o_ready = sem("gate_ready"), sem("o_ready")
        gn_sums_ready = sem("gn_sums_ready")
        gn_spread, gn_step, gn_var_ready, gn_coef_step, gn_coef_ready = sem("gn_spread"), sem("gn_step"), sem("gn_var_ready"), sem("gn_coef_step"), sem("gn_coef_ready")
        z_ready, zhi_ready, zlo_ready = sem("z_ready"), sem("zhi_ready"), sem("zlo_ready")
        y_ready, x2_ready = sem("y_ready"), sem("x2_ready")
        h_ready, relu_ready, hsq_ready, hhi_ready, hlo_ready = sem("h_ready"), sem("relu_ready"), sem("hsq_ready"), sem("hhi_ready"), sem("hlo_ready")
        hlo_last_ready = sem("hlo_last_ready")
        ffn_ready, ffn_sb_ready = sem("ffn_ready"), sem("ffn_sb_ready")
        out_ready, last_out_ready = sem("out_ready"), sem("last_out_ready")

        block = ctx.enter_context(nc.Block())

        def need(eng, s, value):
            if not isinstance(value, int) or value > 0:
                eng.wait_ge(s, value)

        def low_split(b):
            return CH - 1 if isinstance(b, int) and b == NB - 1 else CH - 2

        def live(b):
            return not isinstance(b, int) or 0 <= b < NB

        def rows(b, tile=0, tiles=CT):
            if isinstance(b, int):
                return x_all[:, b * N + tile * D:b * N + (tile + tiles) * D]
            return x_all[:, bass.ds(b * N + tile * D, tiles * D)]

        def parts(buffer, b, chunk=0, chunks=CD):
            if isinstance(b, int):
                return buffer[:, (b * CD + chunk) * T:(b * CD + chunk + chunks) * T]
            return buffer[:, bass.ds((b * CD + chunk) * T, chunks * T)]

        def part_tile(buffer, b, chunk, tile):
            at = (b * CD + chunk) * T + tile * P
            return buffer[:, at:at + P] if isinstance(b, int) else buffer[:, bass.ds(at, P)]

        def group(b, chunk=0, chunks=CD):
            return parts(o_all, b, chunk, chunks)

        def run_slots(eng, attention_slot, ffn_slot):
            if attention_slot:
                for i in range(ATTENTION_LOOP[0]):
                    attention_slot(i)
                with eng.Fori(*ATTENTION_LOOP) as i:
                    attention_slot(i)
                for i in range(ATTENTION_LOOP[1], NB):
                    attention_slot(i)
            for j in range(FFN_LOOP[0]):
                ffn_slot(j, j % 2)
            with eng.Fori(FFN_LOOP[0] // 2, FFN_LOOP[1] // 2) as pair:
                ffn_slot(2 * pair, 0)
                ffn_slot(2 * pair + 1, 1)
            for j in range(FFN_LOOP[1], NB + 1):
                ffn_slot(j, j % 2)

        @block.sync
        def _(sp):
            sp.dma_start(x_all[:, 0:N], x[:, 0:N]).then_inc(in_x[0], 16)
            for w in range(3):
                sp.dma_start(w_raw[:, w, :], w_qkv[:, w * CD * D:(w + 1) * CD * D]).then_inc(in_wqkv[w], 16)
            sp.dma_start(x_all[:, N:2 * N], x[:, N:2 * N]).then_inc(in_x[1], 16)
            sp.dma_start(w_raw[:, 3, :], w_out).then_inc(in_wout, 16)
            sp.dma_start(x_all[:, 2 * N:3 * N], x[:, 2 * N:3 * N]).then_inc(in_x[2], 16)
            sp.dma_start(f_raw[:, 0, :], w_fc).then_inc(in_fc, 16)
            sp.dma_start(f_raw[:, 1, :], w_proj).then_inc(in_proj, 16)
            sp.dma_start(x_all[:, 3 * N:NB * N], x[:, 3 * N:NB * N]).then_inc(in_x[3], 16)

            def ffn_slot(j, _):
                b = j - 1
                if isinstance(j, int) and j == NB:
                    for t in range(CT):
                        sp.wait_ge(last_out_ready, t + 1)
                        where = slice(b * N + t * D, b * N + (t + 1) * D)
                        sp.dma_start(out[:, where], x_all[:, where]).then_inc(stored, 16)
                elif live(b):
                    sp.wait_ge(out_ready, b + 1)
                    where = out[:, b * N:(b + 1) * N] if isinstance(b, int) else out[:, bass.ds(b * N, N)]
                    sp.dma_start(where, rows(b)).then_inc(stored, 16)

            run_slots(sp, None, ffn_slot)
            sp.wait_ge(stored, 16 * (NB - 1 + CT))

        @block.tensor
        def _(pe):
            def turn(n, b):
                pe.wait_ge(xn_ready[n], CT * (b + 1))
                if n == 1 and isinstance(b, int) and b == 0:
                    pe.wait_ge(xlo_ready[0], NB)
                else:
                    need(pe, xlo_ready[n], b)
                for c in range(CD):
                    for t in range(CT):
                        last = nc.tensor.transpose(b_turn[:, c * T + t * P:c * T + (t + 1) * P],
                                                   xn[n][:, t * D + c * P:t * D + (c + 1) * P], ident[:])
                last.then_inc(turned[n], 1)

            def project(w, b, dst, ready):
                first = isinstance(b, int) and b == 0
                if first:
                    pe.wait_ge(whi_ready, w + 1)
                for e in range(CD):
                    terms = [(wp, xp, c) for wp, xp in ((w_hi, xt_hi[0]), (w_hi, xt_lo[0]), (w_lo, xt_hi[0]))
                             for c in range(CD)]
                    for j, (wp, xp, c) in enumerate(terms):
                        if first and e == 0 and j == 2 * CD:
                            pe.wait_ge(*((wlo_ready, w + 1) if w < 2 else (wlo_r_ready, 1)))
                        last = nc.tensor.matmul(dst[:, e * T:(e + 1) * T], wp[:, w, c * D + e * P:c * D + (e + 1) * P],
                                                parts(xp, b, c, 1), start=(j == 0), stop=(j == len(terms) - 1))
                last.then_inc(ready, 1)

            def project_k(b):
                pe.wait_ge(xlo_ready[0], b + 1)
                need(pe, kw_ready, b)
                project(0, b, b_k, k_ready)

            def project_v(b):
                need(pe, u_ready, b)
                project(1, b, b_v, v_ready)

            def project_r(b):
                need(pe, gate_ready, b)
                project(2, b, b_r, r_ready)

            def spread_group_stats(b):
                pe.wait_ge(gn_sums_ready, 2 * (b + 1))
                need(pe, gn_step, b)
                nc.tensor.matmul(b_o[:, 0:2], mean_mat[:], gn_sums[:], start=True, stop=True).then_inc(gn_spread, 1)

            def output_product(b):
                pe.wait_ge(wlo_ready, 3)
                pe.wait_ge(zlo_ready, b + 1)
                if y_bank(b) is b_y:
                    need(pe, x2_ready, b)
                for t in range(CT):
                    terms = [(zp, wp, c) for c in range(CD)
                             for zp, wp in ((z_hi, w_hi), (z_hi, w_lo), (z_lo, w_hi))]
                    for j, (zp, wp, c) in enumerate(terms):
                        last = nc.tensor.matmul(y_bank(b)[:, t * D:(t + 1) * D], part_tile(zp, b, c, t),
                                                wp[:, 3, c * D:(c + 1) * D], start=(j == 0), stop=(j == len(terms) - 1))
                last.then_inc(y_ready, 1)

            def hidden_product(b):
                pe.wait_ge(xlo_ready[1], b + 1)
                if isinstance(b, int) and b == 0:
                    pe.wait_ge(fq_ready[0], CH)
                    pe.wait_ge(kw_ready, NB)
                for p, (h0, h1) in enumerate(PAIRS):
                    need(pe, relu_ready, 3 * b + p - 2)
                    for h in range(h0, h1):
                        terms = [(xp, c) for c in range(CD) for xp in (xt_hi[1], xt_lo[1])]
                        for j, (xp, c) in enumerate(terms):
                            last = nc.tensor.matmul(b_h[p][:, (h - h0) * T:(h - h0 + 1) * T],
                                                    f_q[:, 0, c * H + h * P:c * H + (h + 1) * P], parts(xp, b, c, 1),
                                                    start=(j == 0), stop=(j == len(terms) - 1))
                    last.then_inc(h_ready, 1)

            def last_product(b, n):
                pe.wait_ge(hlo_ready, 2 * b + 1)
                apart = isinstance(b, int) and b == NB - 1
                if not apart:
                    need(pe, ffn_sb_ready, b)
                if isinstance(b, int) and b == 0:
                    pe.wait_ge(fq_ready[1], CH)
                    pe.wait_ge(gn_step, NB)
                dst = last_banks if apart else [b_o[:, 0:D], b_o[:, D:2 * D]]

                def chunks(t, h0, h1):
                    for h in range(h0, h1):
                        for hp in (h_hi[n], h_lo[n]):
                            last = nc.tensor.matmul(dst[t], hp[:, h * T + t * P:h * T + (t + 1) * P], f_q[:, 1, h * D:(h + 1) * D],
                                                    start=(h == 0 and hp is h_hi[n]), stop=(h == CH - 1 and hp is h_lo[n]))
                    return last

                def await_others():
                    pe.wait_ge(hlo_ready, 2 * b + 2)
                    pe.wait_ge(hlo_last_ready, b + 1)

                chunks(0, 0, 2)
                if apart:
                    chunks(1, 0, 2)
                await_others()
                chunks(0, 2, CH).then_inc(ffn_ready, 1)
                chunks(1, 2 if apart else 0, CH).then_inc(ffn_ready, 1)

            def turn_weight_max(step, first, count):
                pe.wait_ge(wmax_ready, step)
                nc.tensor.transpose(bank[7][0:count, 0:P], w_max[:, first:first + count], ident[:]).then_inc(wmax_turned, 1)

            def spread_weight_max(step, count):
                pe.wait_ge(wdiag_ready, step)
                nc.tensor.matmul(bank[7][:, P:P + count], ones[0:count, :], w_max_diag[0:count, 4 * step - 4:4 * step - 4 + count],
                                 start=True, stop=True).then_inc(wmax_spread, 1)

            def spread_ffn_sums():
                pe.wait_ge(fsum_ready, 2)
                nc.tensor.matmul(bank[6][:, 256:258], ones[:], f_sum[:], start=True, stop=True).then_inc(fsum_spread, 1)

            def attention_slot(i):
                at = i if isinstance(i, int) else None
                if at not in (0, 1, 2):
                    turn(*((0, i + 1) if live(i + 1) else (1, 0)))
                project_k(i)
                if at in (1, 2):
                    turn(0, i + 1)
                project_v(i)
                if at == 1:
                    turn_weight_max(2, 3, 2)
                if at == 0:
                    turn(0, 1)
                project_r(i)
                if at == 1:
                    spread_weight_max(2, 2)
                    spread_ffn_sums()
                if live(i - 1):
                    spread_group_stats(i - 1)
                if live(i - 3):
                    output_product(i - 3)

            def ffn_slot(j, n):
                at = j if isinstance(j, int) else None
                if live(j):
                    hidden_product(j)
                if at == 1:
                    spread_group_stats(NB - 1)
                if live(j + 1):
                    turn(1, j + 1)
                if at == 0:
                    output_product(NB - 3)
                if live(j - 1):
                    last_product(j - 1, 1 - n)
                if at == 1:
                    output_product(NB - 2)
                    output_product(NB - 1)

            def keep_warm(count):
                for _ in range(count):
                    nc.tensor.matmul(bank[6][:, 0:P], ones[:], ones[:], start=True, stop=True)

            pe.wait_ge(consts_ready, 1)
            keep_warm(WARM_UP[0])
            turn_weight_max(1, 0, 3)
            keep_warm(WARM_UP[1])
            turn(0, 0)
            spread_weight_max(1, 3)
            keep_warm(WARM_UP[2])
            run_slots(pe, attention_slot, ffn_slot)

        @block.vector
        def _(dve):
            steps = [0]

            def step(ins):
                steps[0] += 1
                ins.then_inc(setup_step, 1)
                dve.wait_ge(setup_step, steps[0])


            def layer_stats(n, b, t):
                nc.vector.bn_stats(ln_stats[n][:, t, :], rows(b, t, 1)).then_inc(ln_stats_done[n], 1)

            def await_layer_stats(n, b):
                dve.wait_ge(ln_stats_done[n], CT * (b + 1))
                need(dve, ln_coef_ready[n], b)

            def layer_mean(n, b):
                for t in range(CT):
                    last = nc.vector.bn_aggr(ln_mv[n][:, t, :], ln_stats[n][:, t, :])
                last.then_inc(ln_mv_ready[n], 1)

            def first_stats(b):
                if isinstance(b, int) and b < 4:
                    dve.wait_ge(in_x[b], 16)
                for t in range(CT):
                    layer_stats(0, b, t)

            def low_part(n, b):
                dve.wait_ge(xhi_ready[n], b + 1)
                nc.vector.tensor_tensor(parts(xt_lo[n], b), b_turn[:], parts(xt_hi[n], b),
                                        ALU.subtract).then_inc(xlo_ready[n], 1)

            def weigh_k(b):
                dve.wait_ge(k_ready, b + 1)
                nc.vector.scalar_tensor_tensor(out=kw_sb[:], in0=b_k[:], scalar=unscale[:, 0:1], in1=kv_weight[:],
                                               op0=ALU.mult, op1=ALU.mult).then_inc(kw_ready, 1)

            def kv(b):
                dve.wait_ge(v_ready, b + 1)
                dve.wait_ge(kw_ready, b + 1)
                nc.vector.tensor_tensor(u_sb[:].rearrange("p c t -> p (c t)"), b_v[:], kw_sb[:], ALU.mult).then_inc(u_ready, 1)

            def scan(b, c):
                dve.wait_ge(u_ready, b + 1)
                need(dve, o_ready, b)
                nc.vector.tensor_tensor_scan(state[:, c, :], d_keep[:, c:c + 1].to_broadcast([P, T]),
                                             u_sb[:, c, :], 0.0, ALU.mult, ALU.add).then_inc(scan_ready, 1)

            def group_copy(b):
                dve.wait_ge(gn_spread, b + 1)
                need(dve, gn_coef_ready, b)
                nc.vector.tensor_copy(gn_all[:], b_o[:, 0:2]).then_inc(gn_step, 1)

            def group_variance(b):
                dve.wait_ge(gn_step, b + 1)
                nc.vector.scalar_tensor_tensor(out=gn_nvar[:], in0=gn_all[:, 0:1], scalar=gn_all[:, 0:1],
                                               in1=gn_all[:, 1:2], op0=ALU.mult, op1=ALU.add).then_inc(gn_var_ready, 1)

            def group_eps(b):
                dve.wait_ge(gn_var_ready, 2 * b + 1)
                nc.vector.tensor_scalar(gn_nveps[:], gn_nvar[:], 0.0, EPS, ALU.min,
                                        ALU.subtract).then_inc(gn_var_ready, 1)

            def add_attention(b):
                dve.wait_ge(y_ready, b + 1)
                nc.vector.scalar_tensor_tensor(out=rows(b), in0=y_bank(b)[:], scalar=y_unscale[:], in1=rows(b),
                                               op0=ALU.mult, op1=ALU.add).then_inc(x2_ready, 1)

            def z_low(b):
                dve.wait_ge(zhi_ready, b + 1)
                nc.vector.tensor_tensor(parts(z_lo, b), z_sb[:], parts(z_hi, b), ALU.subtract).then_inc(zlo_ready, 1)

            def square(b, part):
                c0, c2 = ((0, 2), (2, CH))[part]
                dve.wait_ge(relu_ready, 3 * b + (1, 3)[part])
                if part:
                    need(dve, hlo_last_ready, b)
                nc.vector.tensor_tensor(h_sq[:, c0 * T:c2 * T], h_relu[:, c0 * T:c2 * T], h_relu[:, c0 * T:c2 * T],
                                        ALU.mult).then_inc(hsq_ready, 1)

            def square_low(b, part, n):
                c0, c1 = ((0, 2), (2, low_split(b)))[part]
                dve.wait_ge(hsq_ready, 2 * b + part + 1)
                dve.wait_ge(hhi_ready, 2 * b + part + 1)
                need(dve, ffn_ready, CT * (b - 1))
                nc.vector.tensor_tensor(h_lo[n][:, c0 * T:c1 * T], h_sq[:, c0 * T:c1 * T], h_hi[n][:, c0 * T:c1 * T],
                                        ALU.subtract).then_inc(hlo_ready, 1)

            def weight_max(w, src):
                return nc.vector.tensor_reduce(w_max[:, w:w + 1], src, AX.X, ALU.max, apply_absolute_value=True)

            def gather_weight_max(n, count):
                dve.wait_ge(wmax_turned, n)
                step(nc.vector.tensor_reduce(w_max_all[0:count, n - 1:n], bank[7][0:count, 0:P], AX.X, ALU.max))
                nc.vector.tensor_scalar(w_max_diag[0:count, 4 * n - 4:4 * n - 4 + count], ident[0:count, 0:count],
                                        w_max_all[0:count, n - 1:n], None, ALU.mult).then_inc(wdiag_ready, 1)

            def weight_scale(n, w0, w1):
                dve.wait_ge(wmax_spread, n)
                step(nc.vector.tensor_scalar(w_pow[:, w0:w1], bank[7][:, P:P + w1 - w0], 1e-30, None, ALU.max))
                step(nc.vector.tensor_scalar(w_pow[:, w0:w1].bitcast(U32), w_pow[:, w0:w1].bitcast(U32), EXPONENT, None,
                                             ALU.bitwise_and))
                step(nc.vector.reciprocal(w_inv[:, w0:w1], w_pow[:, w0:w1]))
                nc.vector.tensor_scalar(w_mul[:, w0:w1], w_inv[:, w0:w1], W_SCALE, None, ALU.mult).then_inc(wscale_ready, 1)
                nc.vector.tensor_scalar(unscale[:, w0:w1], w_pow[:, w0:w1], 1.0 / (W_SCALE * X_SCALE), None,
                                        ALU.mult).then_inc(unscale_ready, 1)

            def weight_low(w, src):
                dve.wait_ge(whi_ready, w + 1)
                nc.vector.scalar_tensor_tensor(out=w_lo[:, w, :], in0=src, scalar=w_mul[:, w:w + 1],
                                               in1=w_hi[:, w, :], op0=ALU.mult, op1=ALU.subtract).then_inc(wlo_ready, 1)

            def ternary_scales():
                dve.wait_ge(fsum_spread, 1)
                step(nc.vector.tensor_scalar(f_mean[:], bank[6][:, 256:258], 1.0 / (D * H), 1e-5, ALU.mult, ALU.max))
                nc.vector.tensor_scalar(f_thr[:], f_mean[:], 0.7, None, ALU.mult)
                step(nc.vector.tensor_tensor(f_m2[:], f_mean[:, 0:1], f_mean[:, 0:1], ALU.mult))
                nc.vector.tensor_scalar(f_nthr[:], f_thr[:], -1.0, None, ALU.mult).then_inc(fthr_ready, 1)
                nc.vector.tensor_scalar(f_unscale[:], f_m2[:], f_mean[:, 1:2], 1.0 / H_SCALE ** 2, ALU.mult,
                                        ALU.mult).then_inc(funscale_ready, 1)

            def columns_of(piece):
                return slice(piece * T, (piece + 1) * T) if isinstance(piece, int) else bass.ds(piece * T, T)

            def below(w, piece):
                dve.wait_ge(fthr_ready, 1)
                nc.vector.tensor_scalar(f_neg[:, w, columns_of(piece)], f_raw[:, w, columns_of(piece)], f_nthr[:, w:w + 1],
                                        None, ALU.is_lt).then_inc(fneg_ready[w], 1)

            def ternary(w, piece):
                where = columns_of(piece)
                dve.wait_ge(fneg_ready[w], piece + 1)
                nc.vector.scalar_tensor_tensor(out=f_q[:, w, where], in0=f_raw[:, w, where], scalar=f_thr[:, w:w + 1],
                                               in1=f_neg[:, w, where], op0=ALU.is_gt, op1=ALU.subtract).then_inc(fq_ready[w], 1)

            def decay_power(c):
                nc.vector.tensor_tensor_scan(d_power[:, c, 1:], d_keep[:, c:c + 1].to_broadcast([P, T - 1]),
                                             zeros[:, 1:], 1e10, ALU.mult, ALU.add).then_inc(dpower_ready, 1)

            def normalise(n, b, first_tile=0):
                dve.wait_ge(ln_coef_ready[n], b + 1)
                need(dve, turned[n], b)
                for t in range(first_tile, CT):
                    nc.vector.tensor_scalar(xn[n][:, t * D:(t + 1) * D], rows(b, t, 1), ln_rs[n][:, t:t + 1],
                                            ln_bias[n][:, t:t + 1], ALU.mult, ALU.add).then_inc(xn_ready[n], 1)

            dve.wait_ge(dsig_ready, 1)
            step(nc.vector.tensor_scalar(d_keep[:], d_sig[:], 1e-7, None, ALU.max))
            dve.wait_ge(consts_ready, 1)
            decay_power(0)
            first_stats(0)
            await_layer_stats(0, 0)
            layer_mean(0, 0)
            for w in range(3):
                dve.wait_ge(in_wqkv[w], 16)
                last = weight_max(w, w_raw[:, w, :])
            last.then_inc(wmax_ready, 1)
            normalise(0, 0, first_tile=1)
            gather_weight_max(1, 3)
            dve.wait_ge(ln_mv_ready[0], 1)
            first_stats(1)
            weight_scale(1, 0, 3)
            low_part(0, 0)
            await_layer_stats(0, 1)
            layer_mean(0, 1)
            for w in range(2):
                weight_low(w, w_raw[:, w, :])
            dve.wait_ge(ln_mv_ready[0], 2)
            first_stats(2)
            decay_power(1)
            await_layer_stats(0, 2)
            layer_mean(0, 2)
            dve.wait_ge(dpower_ready, CD)
            nc.vector.tensor_scalar(kv_weight[:], d_power[:].rearrange("p c t -> p (c t)"), 1.0, unscale[:, 1:2],
                                    ALU.min, ALU.mult).then_inc(kvweight_ready, 1)

            def attention_slot(i):
                at = i if isinstance(i, int) else None
                n, ahead = (0, i + 2) if live(i + 2) else (1, i + 2 - NB)
                if at == 1:
                    dve.wait_ge(in_x[ahead], 16)
                if n == 1:
                    dve.wait_ge(x2_ready, ahead + 1)
                if at != 0:
                    for t in range(CT):
                        layer_stats(n, ahead, t)
                    await_layer_stats(n, ahead)
                if live(i - 2):
                    group_copy(i - 2)
                if at != 0:
                    layer_mean(n, ahead)
                if at == 2:
                    weight_scale(2, 3, 5)
                if at == 0:
                    dve.wait_ge(kvweight_ready, 1)
                    weigh_k(i)
                low_part(*((0, i + 1) if live(i + 1) else (1, 0)))
                if live(i - 2):
                    group_variance(i - 2)
                if at != 0:
                    weigh_k(i)
                if live(i - 2):
                    group_eps(i - 2)
                if at == 1:
                    gather_weight_max(2, 2)
                if live(i - 3):
                    below(0, i - 3)
                    below(1, i - 3)
                kv(i)
                if live(i - 3):
                    ternary(0, i - 3)
                for c in range(CD):
                    scan(i, c)
                if live(i - 3):
                    ternary(1, i - 3)
                if at == NB - 1:
                    dve.wait_ge(gate_ready, NB)
                    dve.wait_ge(scan_ready, CD * NB)
                    nc.vector.tensor_tensor(group(at), gate[:], state[:].rearrange("p c t -> p (c t)"),
                                            ALU.mult).then_inc(o_ready, 1)
                if live(i - 3):
                    add_attention(i - 3)
                if at == 0:
                    dve.wait_ge(in_wout, 16)
                    weight_max(3, w_raw[:, 3, :])
                    dve.wait_ge(in_cols, 16)
                    nc.vector.tensor_reduce(gn_w_max[:], gn_w_c, AX.X, ALU.max, apply_absolute_value=True)
                    step(nc.vector.tensor_reduce(gn_b_max[:], gn_b_c, AX.X, ALU.max, apply_absolute_value=True))
                    nc.vector.tensor_scalar(w_max[:, 4:5], gn_w_max[:], Z_MAX, gn_b_max[:], ALU.mult,
                                            ALU.add).then_inc(wmax_ready, 1)
                if at == 2:
                    dve.wait_ge(unscale_ready, 2)
                    nc.vector.tensor_scalar(y_unscale[:], unscale[:, 3:4], unscale[:, 4:5], X_SCALE ** 2, ALU.mult, ALU.mult)
                if at == 2:
                    ternary_scales()
                    weight_low(3, w_raw[:, 3, :])

            def ffn_slot(j, n):
                at = j if isinstance(j, int) else None
                if at == 0:
                    group_copy(NB - 2)
                if at == 1:
                    z_low(NB - 2)
                    add_attention(NB - 3)
                if live(j + 2):
                    dve.wait_ge(x2_ready, NB if at is None else at + 3)
                    layer_stats(1, j + 2, 0)
                    if at == 0:
                        group_variance(NB - 2)
                    layer_stats(1, j + 2, 1)
                    if at == 0:
                        group_eps(NB - 2)
                    await_layer_stats(1, j + 2)
                if live(j):
                    square(j, 0)
                if live(j + 2):
                    layer_mean(1, j + 2)
                if live(j):
                    square_low(j, 0, n)
                if at == 1:
                    z_low(NB - 1)
                if live(j + 1):
                    low_part(1, j + 1)
                if live(j):
                    square(j, 1)
                if at == 0:
                    normalise(1, 2)
                if live(j):
                    square_low(j, 1, n)
                if at == 0:
                    group_copy(NB - 1)
                    group_variance(NB - 1)
                if at == 0:
                    group_eps(NB - 1)
                if at == 1:
                    add_attention(NB - 2)
                    add_attention(NB - 1)
                if at == NB:
                    for t, got in enumerate(last_banks):
                        dve.wait_ge(ffn_ready, CT * (NB - 1) + t + 1)
                        nc.vector.scalar_tensor_tensor(out=rows(NB - 1, t, 1), in0=got, scalar=f_unscale[:],
                                                       in1=rows(NB - 1, t, 1), op0=ALU.mult, op1=ALU.add).then_inc(last_out_ready, 1)

            run_slots(dve, attention_slot, ffn_slot)

        @block.scalar
        def _(act):
            def normalise(n, b, tiles=CT):
                act.wait_ge(ln_coef_ready[n], b + 1)
                need(act, turned[n], b)
                for t in range(tiles):
                    nc.scalar.activation(xn[n][:, t * D:(t + 1) * D], rows(b, t, 1), ACT.Identity,
                                         bias=ln_bias[n][:, t:t + 1], scale=ln_rs[n][:, t:t + 1]).then_inc(xn_ready[n], 1)

            def high_part(n, b):
                act.wait_ge(turned[n], b + 1)
                nc.scalar.activation(parts(xt_hi[n], b), b_turn[:], ACT.Copy).then_inc(xhi_ready[n], 1)

            def gate_of(b):
                act.wait_ge(r_ready, b + 1)
                need(act, o_ready, b)
                nc.scalar.activation(gate[:], b_r[:], ACT.Sigmoid, scale=unscale[:, 2:3]).then_inc(gate_ready, 1)

            def group_sums(b):
                act.wait_ge(o_ready, b + 1)
                need(act, gn_spread, b)
                for n, function in enumerate((ACT.Copy, ACT.Square)):
                    nc.scalar.activation(gn_copies[n][:], group(b), function,
                                         accum_out=gn_sums[:, n:n + 1]).then_inc(gn_sums_ready, 1)

            def group_normalise(b):
                act.wait_ge(gn_coef_ready, b + 1)
                need(act, zlo_ready, b)
                for c in range(CD):
                    nc.scalar.activation(z_sb[:, c * T:(c + 1) * T], group(b, c, 1), ACT.Identity,
                                         bias=gn_bias[:, c:c + 1], scale=gn_scale[:, c:c + 1]).then_inc(z_ready, 1)

            def z_high(b):
                act.wait_ge(z_ready, CD * (b + 1))
                nc.scalar.activation(parts(z_hi, b), z_sb[:], ACT.Copy).then_inc(zhi_ready, 1)

            def relu(b, p):
                h0, h1 = PAIRS[p]
                act.wait_ge(h_ready, 3 * b + p + 1)
                need(act, hsq_ready, 2 * b)
                nc.scalar.activation(h_relu[:, h0 * T:h1 * T], b_h[p][:, 0:(h1 - h0) * T], ACT.Relu,
                                     scale=H_SCALE / X_SCALE).then_inc(relu_ready, 1)

            def square_high(b, part, n):
                c0, c1 = ((0, 2), (2, CH))[part]
                act.wait_ge(relu_ready, 3 * b + (1, 3)[part])
                need(act, ffn_ready, CT * (b - 1))
                nc.scalar.activation(h_hi[n][:, c0 * T:c1 * T], h_relu[:, c0 * T:c1 * T], ACT.Square).then_inc(hhi_ready, 1)

            def copy_ffn(b):
                act.wait_ge(ffn_ready, CT * (b + 1))
                need(act, out_ready, b)
                nc.scalar.activation(ffn_out[:], b_o[:], ACT.Copy, scale=f_unscale[:]).then_inc(ffn_sb_ready, 1)

            def weight_high(w, src):
                nc.scalar.activation(w_hi[:, w, :], src, ACT.Copy, scale=w_mul[:, w:w + 1]).then_inc(whi_ready, 1)

            act.dma_start(cols[:], columns).then_inc(in_cols, 16)
            act.wait_ge(in_cols, 16)
            nc.scalar.activation(d_sig[:], decay_c, ACT.Sigmoid).then_inc(dsig_ready, 1)
            normalise(0, 0, tiles=1)
            high_part(0, 0)
            act.wait_ge(wscale_ready, 1)
            for w in range(3):
                weight_high(w, w_raw[:, w, :])
            normalise(0, 1)

            def sum_magnitudes(w):
                act.wait_ge((in_fc, in_proj)[w], 16)
                if w:
                    act.wait_ge(fsum_ready, 1)
                nc.scalar.activation(f_abs[:], f_raw[:, w, :], ACT.Abs, accum_out=f_sum[:, w:w + 1]).then_inc(fsum_ready, 1)

            def attention_slot(i):
                at = i if isinstance(i, int) else None
                if live(i + 1):
                    high_part(0, i + 1)
                else:
                    high_part(1, 0)
                if at in (0, 1):
                    sum_magnitudes(at)
                if live(i - 3):
                    group_normalise(i - 3)
                    z_high(i - 3)
                if live(i - 1):
                    group_sums(i - 1)
                if live(i + 2):
                    normalise(0, i + 2)
                else:
                    normalise(1, i + 2 - NB)
                gate_of(i)
                if at == 2:
                    act.wait_ge(wscale_ready, 2)
                    weight_high(3, w_raw[:, 3, :])

            def ffn_slot(j, n):
                at = j if isinstance(j, int) else None
                if at == 0:
                    z_high(NB - 3)
                if live(j):
                    relu(j, 0)
                    square_high(j, 0, n)
                    relu(j, 1)
                    relu(j, 2)
                if live(j + 1):
                    high_part(1, j + 1)
                if at == 0:
                    group_sums(NB - 1)
                if live(j):
                    square_high(j, 1, n)
                if at == 1:
                    z_high(NB - 1)
                if at != 0 and live(j + 2):
                    normalise(1, j + 2)
                if at == 0:
                    z_high(NB - 2)
                if live(j - 1) and at != NB:
                    if at == 1:
                        act.wait_ge(funscale_ready, 1)
                    copy_ffn(j - 1)

            run_slots(act, attention_slot, ffn_slot)

        @block.gpsimd
        def _(pool):
            def layer_coefficients(n, b):
                need(pool, xn_ready[n], CT * b)
                pool.wait_ge(ln_mv_ready[n], b + 1)
                nc.gpsimd.tensor_tensor(ln_nm[n][:], ln_mv[n][:, :, 0], minus_one[:], ALU.mult).then_inc(ln_step[n], 1)
                nc.gpsimd.tensor_scalar(ln_var[n][:], ln_mv[n][:, :, 1], X_SCALE ** -2, EPS * X_SCALE ** -2,
                                        ALU.mult, ALU.add).then_inc(ln_step[n], 1)
                pool.wait_ge(ln_step[n], 3 * b + 2)
                nc.gpsimd.tensor_tensor(ln_rs[n][:], ln_var[n][:], minus_half[:], ALU.pow).then_inc(ln_step[n], 1)
                pool.wait_ge(ln_step[n], 3 * b + 3)
                nc.gpsimd.tensor_tensor(ln_bias[n][:], ln_nm[n][:], ln_rs[n][:], ALU.mult).then_inc(ln_coef_ready[n], 1)

            def group_coefficients(b):
                need(pool, z_ready, CD * b)
                pool.wait_ge(gn_var_ready, 2 * b + 2)
                nc.gpsimd.tensor_tensor(gn_veps[:], gn_nveps[:], minus_one[:, 0:1], ALU.mult).then_inc(gn_coef_step, 1)
                pool.wait_ge(gn_coef_step, 4 * b + 1)
                nc.gpsimd.tensor_tensor(gn_rs[:], gn_veps[:], minus_half[:, 0:1], ALU.pow).then_inc(gn_coef_step, 1)
                pool.wait_ge(gn_coef_step, 4 * b + 2)
                nc.gpsimd.tensor_tensor(gn_scale[:], gn_wz[:], gn_rs[:].to_broadcast([P, CD]), ALU.mult).then_inc(gn_coef_step, 1)
                pool.wait_ge(gn_coef_step, 4 * b + 3)
                nc.gpsimd.tensor_tensor(gn_shift[:], gn_scale[:], gn_all[:, 0:1].to_broadcast([P, CD]), ALU.mult).then_inc(gn_coef_step, 1)
                pool.wait_ge(gn_coef_step, 4 * b + 4)
                nc.gpsimd.tensor_tensor(gn_bias[:], gn_shift[:], gn_bz[:], ALU.add).then_inc(gn_coef_ready, 1)

            def gate_state(b):
                pool.wait_ge(gate_ready, b + 1)
                pool.wait_ge(scan_ready, CD * (b + 1))
                nc.gpsimd.tensor_tensor(group(b), gate[:], state[:].rearrange("p c t -> p (c t)"), ALU.mult).then_inc(o_ready, 1)

            def group_normalise(b):
                pool.wait_ge(gn_coef_ready, b + 1)
                pool.wait_ge(zlo_ready, b)
                for c in range(CD):
                    nc.gpsimd.tensor_scalar(z_sb[:, c * T:(c + 1) * T], group(b, c, 1), gn_scale[:, c:c + 1],
                                            gn_bias[:, c:c + 1], ALU.mult, ALU.add).then_inc(z_ready, 1)

            def z_low(b):
                pool.wait_ge(zhi_ready, b + 1)
                nc.gpsimd.tensor_tensor(parts(z_lo, b), z_sb[:], parts(z_hi, b), ALU.subtract).then_inc(zlo_ready, 1)

            def last_low(b, n):
                pool.wait_ge(hsq_ready, 2 * b + 2)
                pool.wait_ge(hhi_ready, 2 * b + 2)
                need(pool, ffn_ready, CT * (b - 1))
                c = low_split(b) * T
                nc.gpsimd.tensor_tensor(h_lo[n][:, c:], h_sq[:, c:], h_hi[n][:, c:], ALU.subtract).then_inc(hlo_last_ready, 1)

            def add_ffn(b):
                pool.wait_ge(ffn_sb_ready, b + 1)
                nc.gpsimd.tensor_tensor(rows(b), rows(b), ffn_out[:], ALU.add).then_inc(out_ready, 1)

            nc.gpsimd.memset(ident[:], 0.0).then_inc(consts_step, 1)
            pool.wait_ge(consts_step, 1)
            nc.gpsimd.affine_select(out=ident[:], in_=ident[:], compare_op=ALU.not_equal, fill=1.0, base=0,
                                    pattern=[[-1, P]], channel_multiplier=1)
            nc.gpsimd.memset(minus_half[:], -0.5)
            nc.gpsimd.memset(minus_one[:], -1.0)
            nc.gpsimd.memset(ones[:], 1.0)
            nc.gpsimd.memset(mean_mat[:], -1.0 / (P * N))
            nc.gpsimd.memset(zeros[:], 0.0)
            nc.gpsimd.memset(d_power[:, :, 0:1], 1e10).then_inc(consts_ready, 1)
            pool.wait_ge(consts_ready, 1)
            layer_coefficients(0, 0)
            layer_coefficients(0, 1)
            pool.wait_ge(whi_ready, 3)
            nc.gpsimd.tensor_scalar(wr_scaled[:], w_raw[:, 2, :], w_mul[:, 2:3], 0.0, ALU.mult, ALU.add).then_inc(wr_scaled_ready, 1)
            pool.wait_ge(wr_scaled_ready, 1)
            nc.gpsimd.tensor_tensor(w_lo[:, 2, :], wr_scaled[:], w_hi[:, 2, :], ALU.subtract).then_inc(wlo_r_ready, 1)

            def attention_slot(i):
                at = i if isinstance(i, int) else None
                if live(i - 1):
                    gate_state(i - 1)
                if live(i + 2):
                    layer_coefficients(0, i + 2)
                else:
                    layer_coefficients(1, i + 2 - NB)
                if at == 2:
                    pool.wait_ge(wscale_ready, 2)
                    for wide, narrow in ((gn_wz, gn_w_c), (gn_bz, gn_b_c)):
                        nc.gpsimd.tensor_tensor(wide[:], narrow, w_mul[:, 4:5].to_broadcast([P, CD]),
                                                ALU.mult).then_inc(gnaffine_ready, 1)
                    pool.wait_ge(gnaffine_ready, 2)
                if live(i - 3):
                    z_low(i - 3)
                if live(i - 2):
                    group_coefficients(i - 2)

            def ffn_slot(j, n):
                at = j if isinstance(j, int) else None
                if at == 0:
                    group_normalise(NB - 3)
                    z_low(NB - 3)
                if at == 0:
                    group_coefficients(NB - 2)
                    layer_coefficients(1, 2)
                    group_normalise(NB - 2)
                if at == 1:
                    group_coefficients(NB - 1)
                    group_normalise(NB - 1)
                if at != 0 and live(j + 2):
                    layer_coefficients(1, j + 2)
                if live(j):
                    last_low(j, n)
                if live(j - 1) and at != NB:
                    add_ffn(j - 1)

            run_slots(pool, attention_slot, ffn_slot)


def kernel(L0_attn_x, L0_attn_Wr, L0_attn_Wk, L0_attn_Wv, L0_attn_Wo, L0_attn_decay, L0_attn_gn_weight,
           L0_attn_gn_bias, L0_ffn_w_fc, L0_ffn_w_proj):
    import concourse.bacc as bacc
    from concourse.bass_utils import run_bass_kernel_spmd

    def by_partition(a):
        a = np.asarray(a)
        a = a.reshape(a.shape[0] // P, P, -1)
        return np.ascontiguousarray(a.transpose(1, 0, 2).reshape(P, -1))

    B, T, D = L0_attn_x.shape
    arrays = {
        "in_x": by_partition(np.asarray(L0_attn_x).reshape(B * T, D)),
        "in_w_qkv": np.ascontiguousarray(np.concatenate([by_partition(np.asarray(w).T) for w in (L0_attn_Wk, L0_attn_Wv, L0_attn_Wr)], axis=1)),
        "in_w_out": by_partition(np.asarray(L0_attn_Wo).T),
        "in_columns": np.ascontiguousarray(np.concatenate(
            [by_partition(np.asarray(a).reshape(-1, 1)) for a in (L0_attn_decay, L0_attn_gn_weight, L0_attn_gn_bias)], axis=1)),
        "in_w_fc": by_partition(np.asarray(L0_ffn_w_fc).T),
        "in_w_proj": by_partition(np.asarray(L0_ffn_w_proj).T),
    }
    nc = bacc.Bacc("TRN2", target_bir_lowering=False, num_devices=1)
    args = [nc.dram_tensor(n, a.shape, mybir.dt.from_np(a.dtype), kind="ExternalInput").ap() for n, a in arrays.items()]
    result = nc.dram_tensor("result", arrays["in_x"].shape, mybir.dt.float32, kind="ExternalOutput").ap()
    decay_block_kernel(nc, *args, result)
    r = run_bass_kernel_spmd(nc, [arrays], core_ids=[0])
    got = r.results[0]["result"].reshape(P, B * T // P, D)
    return np.ascontiguousarray(got.transpose(1, 0, 2)).reshape(B, T, D)
```

```python
import numpy as np
import concourse.bass as bass
from concourse import mybir
from contextlib import ExitStack

P = 128


def decay_block_kernel(nc, x, w_qkv, w_out, columns, w_fc, w_proj, out):
    F32, F16, U32 = mybir.dt.float32, mybir.dt.float16, mybir.dt.uint32
    ALU, ACT = mybir.AluOpType, mybir.ActivationFunctionType

    D = 256
    NB = 8
    T = x.shape[1] // NB // D * P
    CD, CT = D // P, T // P
    N = CT * D
    H = w_fc.shape[1] // CD
    CH = H // P
    assert T == D and N == 512
    assert CD * H == CH * D == (NB - 3) * T
    EPS = 1e-5
    EXPONENT = 0x7F800000

    X_SCALE = 2.0 ** 8
    Z_MAX = float(np.sqrt(T * D))
    W_SCALE = 2.0 ** 14
    H_SCALE = 2.0 ** -1
    WARM_UP = (11, 4)
    ATTENTION_LOOP = (3, NB - 2)
    FFN_LOOP = (2, NB - 2)

    PAIRS = [(0, 2), (2, 4), (4, CH)]

    ctx = ExitStack()
    with ctx:
        def sb(name, shape, dt):
            return ctx.enter_context(nc.sbuf_tensor(name, shape, dt))

        def sem(name):
            return ctx.enter_context(nc.semaphore(name))

        ident = sb("ident", [P, P], F32)
        ones = sb("ones", [P, P], F32)
        mean_mat = sb("mean_mat", [P, P], F32)
        minus_half = sb("minus_half", [P, CT], F32)
        minus_one = sb("minus_one", [P, CT], F32)
        zeros = sb("zeros", [P, T], F32)
        cols = sb("cols", [P, 3 * CD], F32)
        decay_c, gn_w_c, gn_b_c = cols[:, 0:CD], cols[:, CD:2 * CD], cols[:, 2 * CD:3 * CD]
        w_raw = sb("w_raw", [P, 4, CD * D], F32)
        w_hi = sb("w_hi", [P, 4, CD * D], F16)
        w_lo = sb("w_lo", [P, 4, CD * D], F16)
        w_scaled = sb("w_scaled", [P, 2, CD * D], F32)
        w_squares = sb("w_squares", [P, 4 * CD * D + 2 * CD], F32)
        w_sums = sb("w_sums", [P, 5], F32)
        w_root = sb("w_root", [P, 5], F32)
        w_range = sb("w_range", [P, 5], F32)
        w_mul = sb("w_mul", [P, 5], F32)
        unscale = sb("unscale", [P, 5], F32)
        gn_wz = sb("gn_wz", [P, CD], F32)
        gn_bz = sb("gn_bz", [P, CD], F32)
        y_unscale = sb("y_unscale", [P, 1], F32)
        d_sig = sb("d_sig", [P, CD], F32)
        d_keep = sb("d_keep", [P, CD], F32)
        d_power = sb("d_power", [P, CD, T], F32)
        kv_weight = sb("kv_weight", [P, CD * T], F32)
        f_raw = sb("f_raw", [P, 2, CD * H], F32)
        f_abs = sb("f_abs", [P, 2, CD * H], F32)
        f_sum = sb("f_sum", [P, 2, 2], F32)
        f_mean = sb("f_mean", [P, 2], F32)
        f_thr = sb("f_thr", [P, 2], F32)
        f_nthr = sb("f_nthr", [P, 2], F32)
        f_neg = sb("f_neg", [P, 2, CD * H], F16)
        f_q = sb("f_q", [P, 2, CD * H], F16)
        f_mean_sq = sb("f_mean_sq", [P, 1], F32)
        f_unscale = sb("f_unscale", [P, 1], F32)

        x_all = sb("x_all", [P, NB * N], F32)
        ln_stats = [sb(f"ln{n}_stats", [P, CT, 6], F32) for n in (1, 2)]
        ln_mv = [sb(f"ln{n}_mv", [P, CT, 2], F32) for n in (1, 2)]
        ln_var = [sb(f"ln{n}_var", [P, CT], F32) for n in (1, 2)]
        ln_nm = [sb(f"ln{n}_nm", [P, CT], F32) for n in (1, 2)]
        ln_rs = [sb(f"ln{n}_rs", [P, CT], F32) for n in (1, 2)]
        ln_bias = [sb(f"ln{n}_bias", [P, CT], F32) for n in (1, 2)]
        xn = [sb(f"xn{n}", [P, N], F32) for n in (1, 2)]
        xt_hi = [sb(f"xt{n}_hi", [P, NB * CD * T], F16) for n in (1, 2)]
        xt_lo = [sb(f"xt{n}_lo", [P, NB * CD * T], F16) for n in (1, 2)]
        kw_sb = sb("kw_sb", [P, N], F32)
        u_sb = sb("u_sb", [P, CD, T], F32)
        state = sb("state", [P, CD, T], F32)
        gate = sb("gate", [P, N], F32)
        o_all = sb("o_all", [P, NB * N], F32)
        gn_sums = sb("gn_sums", [P, 2], F32)
        gn_copies = [sb(f"gn_{what}", [P, N], F32) for what in ("same", "squared")]
        gn_all = sb("gn_all", [P, 2], F32)
        gn_nvar = sb("gn_nvar", [P, 1], F32)
        gn_nveps = sb("gn_nveps", [P, 1], F32)
        gn_veps = sb("gn_veps", [P, 1], F32)
        gn_rs = sb("gn_rs", [P, 1], F32)
        gn_scale = sb("gn_scale", [P, CD], F32)
        gn_shift = sb("gn_shift", [P, CD], F32)
        gn_bias = sb("gn_bias", [P, CD], F32)
        z_sb = sb("z_sb", [P, N], F32)
        z_last = sb("z_last", [P, N], F32)
        z_hi = sb("z_hi", [P, NB * CD * T], F16)
        z_lo = sb("z_lo", [P, NB * CD * T], F16)
        h_relu = sb("h_relu", [P, CH * T], F32)
        h_sq = sb("h_sq", [P, CH * T], F32)
        h_hi = [sb(f"h_hi{n}", [P, CH * T], F16) for n in range(2)]
        h_lo = [sb(f"h_lo{n}", [P, CH * T], F16) for n in range(2)]
        ffn_out = sb("ffn_out", [P, N], F32)

        bank = [ctx.enter_context(nc.psum_tensor(f"bank_{n}", [P, 512], F32))
                for n in ("turn", "k", "v", "r", "y", "o", "h0", "h1")]
        b_turn, b_k, b_v, b_r, b_y, b_o = bank[:6]
        b_h = [bank[6], bank[7], b_k]
        last_banks = [b_turn[:, 0:D], b_y[:, 0:D]]

        in_x = [sem("in_x0"), sem("in_x1"), sem("in_x2"), sem("in_x_rest")]
        in_wqkv = [sem("in_wk"), sem("in_wv"), sem("in_wr")]
        in_wout, in_cols = sem("in_wout"), sem("in_cols")
        in_fc, in_proj, stored = sem("in_fc"), sem("in_proj"), sem("stored")
        consts_step, consts_ready = sem("consts_step"), sem("consts_ready")
        setup_step = sem("setup_step")
        wsums_ready, wsums_spread = sem("wsums_ready"), sem("wsums_spread")
        wscale_ready, unscale_ready = sem("wscale_ready"), sem("unscale_ready")
        whi_ready = sem("whi_ready")
        wlo_ready = sem("wlo_ready")
        wscaled_ready, wlo_pool_ready = sem("wscaled_ready"), sem("wlo_pool_ready")
        dsig_ready, dpower_ready, kvweight_ready = sem("dsig_ready"), sem("dpower_ready"), sem("kvweight_ready")
        gnaffine_ready = sem("gnaffine_ready")
        fsum_ready, fsum_spread = sem("fsum_ready"), sem("fsum_spread")
        fthr_ready, funscale_ready = sem("fthr_ready"), sem("funscale_ready")
        fneg_ready = [sem("fneg_fc_ready"), sem("fneg_proj_ready")]
        fq_ready = [sem("fq_fc_ready"), sem("fq_proj_ready")]
        ln_stats_done = [sem("ln1_stats_done"), sem("ln2_stats_done")]
        ln_mv_ready = [sem("ln1_mv_ready"), sem("ln2_mv_ready")]
        ln_step = [sem("ln1_step"), sem("ln2_step")]
        ln_coef_ready = [sem("ln1_coef_ready"), sem("ln2_coef_ready")]
        xn_ready = [sem("xn1_ready"), sem("xn2_ready")]
        turned = [sem("turned1"), sem("turned2")]
        xhi_ready = [sem("xhi1_ready"), sem("xhi2_ready")]
        xlo_ready = [sem("xlo1_ready"), sem("xlo2_ready")]
        k_ready, v_ready, r_ready = sem("k_ready"), sem("v_ready"), sem("r_ready")
        kw_ready, u_ready, scan_ready = sem("kw_ready"), sem("u_ready"), sem("scan_ready")
        gate_ready, o_ready = sem("gate_ready"), sem("o_ready")
        gn_sums_ready, gn_spread, gn_copied = sem("gn_sums_ready"), sem("gn_spread"), sem("gn_copied")
        gn_var_ready, gn_coef_step, gn_coef_ready = sem("gn_var_ready"), sem("gn_coef_step"), sem("gn_coef_ready")
        z_ready, zhi_ready, zlo_ready = sem("z_ready"), sem("zhi_ready"), sem("zlo_ready")
        y_ready, x2_ready = sem("y_ready"), sem("x2_ready")
        h_ready, relu_ready, hsq_ready = sem("h_ready"), sem("relu_ready"), sem("hsq_ready")
        hhi_ready, hlo_ready, hlo_last_ready = sem("hhi_ready"), sem("hlo_ready"), sem("hlo_last_ready")
        ffn_ready, ffn_sb_ready = sem("ffn_ready"), sem("ffn_sb_ready")
        out_ready, last_out_ready = sem("out_ready"), sem("last_out_ready")

        block = ctx.enter_context(nc.Block())

        def need(eng, s, value):
            if not isinstance(value, int) or value > 0:
                eng.wait_ge(s, value)

        def low_split(b):
            return {0: CH, NB - 1: CH - 1}.get(b, CH - 2) if isinstance(b, int) else CH - 2

        def live(b):
            return not isinstance(b, int) or 0 <= b < NB

        def y_bank(b):
            return {NB - 2: b_v, NB - 1: b_r}.get(b, b_y) if isinstance(b, int) else b_y

        def z_of(b):
            return z_last if isinstance(b, int) and b == NB - 1 else z_sb

        def rows(b, tile=0, tiles=CT):
            if isinstance(b, int):
                return x_all[:, b * N + tile * D:b * N + (tile + tiles) * D]
            return x_all[:, bass.ds(b * N + tile * D, tiles * D)]

        def parts(buffer, b, chunk=0, chunks=CD):
            if isinstance(b, int):
                return buffer[:, (b * CD + chunk) * T:(b * CD + chunk + chunks) * T]
            return buffer[:, bass.ds((b * CD + chunk) * T, chunks * T)]

        def part_tile(buffer, b, chunk, tile):
            at = (b * CD + chunk) * T + tile * P
            return buffer[:, at:at + P] if isinstance(b, int) else buffer[:, bass.ds(at, P)]

        def group(b, chunk=0, chunks=CD):
            return parts(o_all, b, chunk, chunks)

        def run_slots(eng, attention_slot, ffn_slot):
            if attention_slot:
                for i in range(ATTENTION_LOOP[0]):
                    attention_slot(i)
                with eng.Fori(*ATTENTION_LOOP) as i:
                    attention_slot(i)
                for i in range(ATTENTION_LOOP[1], NB):
                    attention_slot(i)
            for j in range(FFN_LOOP[0]):
                ffn_slot(j, j % 2)
            with eng.Fori(FFN_LOOP[0] // 2, FFN_LOOP[1] // 2) as pair:
                ffn_slot(2 * pair, 0)
                ffn_slot(2 * pair + 1, 1)
            for j in range(FFN_LOOP[1], NB + 1):
                ffn_slot(j, j % 2)

        @block.sync
        def _(sp):
            sp.dma_start(x_all[:, 0:N], x[:, 0:N]).then_inc(in_x[0], 16)
            for w in range(3):
                sp.dma_start(w_raw[:, w, :], w_qkv[:, w * CD * D:(w + 1) * CD * D]).then_inc(in_wqkv[w], 16)
                if w == 0:
                    sp.dma_start(x_all[:, N:2 * N], x[:, N:2 * N]).then_inc(in_x[1], 16)
            sp.dma_start(w_raw[:, 3, :], w_out).then_inc(in_wout, 16)
            sp.dma_start(x_all[:, 2 * N:3 * N], x[:, 2 * N:3 * N]).then_inc(in_x[2], 16)
            sp.dma_start(f_raw[:, 0, :], w_fc).then_inc(in_fc, 16)
            sp.dma_start(f_raw[:, 1, :], w_proj).then_inc(in_proj, 16)
            sp.dma_start(x_all[:, 3 * N:NB * N], x[:, 3 * N:NB * N]).then_inc(in_x[3], 16)

            def ffn_slot(j, _):
                b = j - 1
                if isinstance(j, int) and j == NB:
                    for t in range(CT):
                        sp.wait_ge(last_out_ready, t + 1)
                        where = slice(b * N + t * D, b * N + (t + 1) * D)
                        sp.dma_start(out[:, where], x_all[:, where]).then_inc(stored, 16)
                elif live(b):
                    sp.wait_ge(out_ready, b + 1)
                    where = out[:, b * N:(b + 1) * N] if isinstance(b, int) else out[:, bass.ds(b * N, N)]
                    sp.dma_start(where, rows(b)).then_inc(stored, 16)

            run_slots(sp, None, ffn_slot)
            sp.wait_ge(stored, 16 * (NB - 1 + CT))

        @block.tensor
        def _(pe):
            def turn(n, b):
                pe.wait_ge(xn_ready[n], CT * (b + 1))
                if n == 1 and isinstance(b, int) and b == 0:
                    pe.wait_ge(xlo_ready[0], NB)
                else:
                    need(pe, xlo_ready[n], b)
                for c in range(CD):
                    for t in range(CT):
                        last = nc.tensor.transpose(b_turn[:, c * T + t * P:c * T + (t + 1) * P],
                                                   xn[n][:, t * D + c * P:t * D + (c + 1) * P], ident[:])
                last.then_inc(turned[n], 1)

            def project(w, b, dst, ready):
                first = isinstance(b, int) and b == 0
                if first:
                    pe.wait_ge(whi_ready, w + 1)
                for e in range(CD):
                    terms = [(wp, xp, c) for wp, xp in ((w_hi, xt_hi[0]), (w_hi, xt_lo[0]), (w_lo, xt_hi[0]))
                             for c in range(CD)]
                    for j, (wp, xp, c) in enumerate(terms):
                        if first and j == 2 * CD and w < 2:
                            pe.wait_ge(wlo_ready, CD * w + e + 1)
                        if first and j == 2 * CD and w == 2 and e == 0:
                            pe.wait_ge(wlo_pool_ready, 1)
                        last = nc.tensor.matmul(dst[:, e * T:(e + 1) * T], wp[:, w, c * D + e * P:c * D + (e + 1) * P],
                                                parts(xp, b, c, 1), start=(j == 0), stop=(j == len(terms) - 1))
                last.then_inc(ready, 1)

            def project_k(b):
                pe.wait_ge(xlo_ready[0], b + 1)
                need(pe, kw_ready, b)
                project(0, b, b_k, k_ready)

            def project_v(b):
                need(pe, u_ready, b)
                project(1, b, b_v, v_ready)

            def project_r(b):
                need(pe, gate_ready, b)
                project(2, b, b_r, r_ready)

            def spread_group_stats(b):
                pe.wait_ge(gn_sums_ready, 2 * (b + 1))
                need(pe, gn_copied, b)
                nc.tensor.matmul(b_o[:, 0:2], mean_mat[:], gn_sums[:], start=True, stop=True).then_inc(gn_spread, 1)

            def output_product(b):
                pe.wait_ge(zlo_ready, b + 1)
                if y_bank(b) is b_y:
                    need(pe, x2_ready, b)
                for t in range(CT):
                    terms = [(zp, wp, c) for c in range(CD)
                             for zp, wp in ((z_hi, w_hi), (z_hi, w_lo), (z_lo, w_hi))]
                    for j, (zp, wp, c) in enumerate(terms):
                        last = nc.tensor.matmul(y_bank(b)[:, t * D:(t + 1) * D], part_tile(zp, b, c, t),
                                                wp[:, 3, c * D:(c + 1) * D], start=(j == 0), stop=(j == len(terms) - 1))
                last.then_inc(y_ready, 1)

            def hidden_product(b):
                pe.wait_ge(xlo_ready[1], b + 1)
                if isinstance(b, int) and b == 0:
                    pe.wait_ge(fq_ready[0], CH)
                    pe.wait_ge(kw_ready, NB)
                for p, (h0, h1) in enumerate(PAIRS):
                    need(pe, relu_ready, 3 * b + p - 2)
                    for h in range(h0, h1):
                        terms = [(xp, c) for c in range(CD) for xp in (xt_hi[1], xt_lo[1])]
                        for j, (xp, c) in enumerate(terms):
                            last = nc.tensor.matmul(b_h[p][:, (h - h0) * T:(h - h0 + 1) * T],
                                                    f_q[:, 0, c * H + h * P:c * H + (h + 1) * P], parts(xp, b, c, 1),
                                                    start=(j == 0), stop=(j == len(terms) - 1))
                    last.then_inc(h_ready, 1)

            def last_product(b, n):
                pe.wait_ge(hlo_ready, 2 * b + 1)
                apart = isinstance(b, int) and b == NB - 1
                if not apart:
                    need(pe, ffn_sb_ready, b)
                if isinstance(b, int) and b == 0:
                    pe.wait_ge(fq_ready[1], CH)
                    pe.wait_ge(gn_copied, NB)
                dst = last_banks if apart else [b_o[:, 0:D], b_o[:, D:2 * D]]

                def chunks(t, h0, h1):
                    for h in range(h0, h1):
                        for hp in (h_hi[n], h_lo[n]):
                            last = nc.tensor.matmul(dst[t], hp[:, h * T + t * P:h * T + (t + 1) * P], f_q[:, 1, h * D:(h + 1) * D],
                                                    start=(h == 0 and hp is h_hi[n]), stop=(h == CH - 1 and hp is h_lo[n]))
                    return last

                def await_others():
                    pe.wait_ge(hlo_ready, 2 * b + 2)
                    need(pe, hlo_last_ready, b)

                chunks(0, 0, 2)
                if apart:
                    chunks(1, 0, 2)
                await_others()
                chunks(0, 2, CH).then_inc(ffn_ready, 1)
                chunks(1, 2 if apart else 0, CH).then_inc(ffn_ready, 1)

            def spread_weight_sums(w0, w1):
                pe.wait_ge(wsums_ready, w1)
                nc.tensor.matmul(bank[7][:, w0:w1], ones[:], w_sums[:, w0:w1], start=True, stop=True).then_inc(wsums_spread, 1)

            def spread_ffn_sums():
                pe.wait_ge(fsum_ready, 4)
                nc.tensor.matmul(bank[6][:, 256:258], ones[:], f_sum[:, 0, :], start=True, stop=False)
                nc.tensor.matmul(bank[6][:, 256:258], ones[:], f_sum[:, 1, :], start=False, stop=True).then_inc(fsum_spread, 1)

            def attention_slot(i):
                at = i if isinstance(i, int) else None
                if at not in (0, 1, 2):
                    turn(*((0, i + 1) if live(i + 1) else (1, 0)))
                project_k(i)
                if at in (0, 1, 2):
                    turn(0, i + 1)
                if at == 2:
                    spread_ffn_sums()
                project_v(i)
                project_r(i)
                if at == 0:
                    spread_weight_sums(3, 5)
                if live(i - 1):
                    spread_group_stats(i - 1)
                if at == 2:
                    pe.wait_ge(wlo_pool_ready, 2)
                if live(i - 3):
                    output_product(i - 3)

            def ffn_slot(j, n):
                at = j if isinstance(j, int) else None
                if at == 1:
                    spread_group_stats(NB - 1)
                if live(j):
                    hidden_product(j)
                if live(j + 1):
                    turn(1, j + 1)
                if at == 0:
                    output_product(NB - 3)
                if live(j - 1):
                    last_product(j - 1, 1 - n)
                if at == 1:
                    output_product(NB - 2)
                    output_product(NB - 1)

            def keep_warm(count):
                for _ in range(count):
                    nc.tensor.matmul(bank[6][:, 0:P], ones[:], ones[:], start=True, stop=True)

            pe.wait_ge(consts_ready, 1)
            keep_warm(WARM_UP[0])
            spread_weight_sums(0, 3)
            turn(0, 0)
            keep_warm(WARM_UP[1])
            run_slots(pe, attention_slot, ffn_slot)

        @block.vector
        def _(dve):
            steps = [0]

            def step(ins):
                steps[0] += 1
                ins.then_inc(setup_step, 1)
                dve.wait_ge(setup_step, steps[0])


            def layer_stats(n, b, t):
                nc.vector.bn_stats(ln_stats[n][:, t, :], rows(b, t, 1)).then_inc(ln_stats_done[n], 1)

            def await_layer_stats(n, b):
                dve.wait_ge(ln_stats_done[n], CT * (b + 1))
                need(dve, ln_coef_ready[n], b)

            def layer_mean(n, b):
                for t in range(CT):
                    last = nc.vector.bn_aggr(ln_mv[n][:, t, :], ln_stats[n][:, t, :])
                last.then_inc(ln_mv_ready[n], 1)

            def first_stats(b):
                if isinstance(b, int) and b < 4:
                    dve.wait_ge(in_x[b], 16)
                for t in range(CT):
                    layer_stats(0, b, t)

            def low_part(n, b):
                dve.wait_ge(xhi_ready[n], b + 1)
                nc.vector.tensor_tensor(parts(xt_lo[n], b), b_turn[:], parts(xt_hi[n], b),
                                        ALU.subtract).then_inc(xlo_ready[n], 1)

            def weigh_k(b):
                dve.wait_ge(k_ready, b + 1)
                nc.vector.scalar_tensor_tensor(out=kw_sb[:], in0=b_k[:], scalar=unscale[:, 0:1], in1=kv_weight[:],
                                               op0=ALU.mult, op1=ALU.mult).then_inc(kw_ready, 1)

            def kv(b):
                dve.wait_ge(v_ready, b + 1)
                dve.wait_ge(kw_ready, b + 1)
                nc.vector.tensor_tensor(u_sb[:].rearrange("p c t -> p (c t)"), b_v[:], kw_sb[:], ALU.mult).then_inc(u_ready, 1)

            def scan(b, c):
                dve.wait_ge(u_ready, b + 1)
                need(dve, o_ready, b)
                nc.vector.tensor_tensor_scan(state[:, c, :], d_keep[:, c:c + 1].to_broadcast([P, T]),
                                             u_sb[:, c, :], 0.0, ALU.mult, ALU.add).then_inc(scan_ready, 1)

            def gate_state(b):
                dve.wait_ge(gate_ready, b + 1)
                dve.wait_ge(scan_ready, CD * (b + 1))
                nc.vector.tensor_tensor(group(b), gate[:], state[:].rearrange("p c t -> p (c t)"),
                                        ALU.mult).then_inc(o_ready, 1)

            def output_unscale():
                dve.wait_ge(unscale_ready, 2)
                nc.vector.tensor_scalar(y_unscale[:], unscale[:, 3:4], unscale[:, 4:5], X_SCALE ** 2, ALU.mult, ALU.mult)

            def group_copy(b):
                dve.wait_ge(gn_spread, b + 1)
                need(dve, gn_coef_ready, b)
                nc.vector.tensor_copy(gn_all[:], b_o[:, 0:2]).then_inc(gn_copied, 1)

            def group_variance(b):
                dve.wait_ge(gn_copied, b + 1)
                nc.vector.scalar_tensor_tensor(out=gn_nvar[:], in0=gn_all[:, 0:1], scalar=gn_all[:, 0:1],
                                               in1=gn_all[:, 1:2], op0=ALU.mult, op1=ALU.add).then_inc(gn_var_ready, 1)

            def group_eps(b):
                dve.wait_ge(gn_var_ready, 2 * b + 1)
                nc.vector.tensor_scalar(gn_nveps[:], gn_nvar[:], 0.0, EPS, ALU.min,
                                        ALU.subtract).then_inc(gn_var_ready, 1)

            def add_attention(b):
                dve.wait_ge(y_ready, b + 1)
                nc.vector.scalar_tensor_tensor(out=rows(b), in0=y_bank(b)[:], scalar=y_unscale[:], in1=rows(b),
                                               op0=ALU.mult, op1=ALU.add).then_inc(x2_ready, 1)

            def z_low(b):
                dve.wait_ge(zhi_ready, b + 1)
                nc.vector.tensor_tensor(parts(z_lo, b), z_of(b)[:], parts(z_hi, b), ALU.subtract).then_inc(zlo_ready, 1)

            def square(b, part):
                c0, c2 = ((0, 2), (2, CH))[part]
                dve.wait_ge(relu_ready, 3 * b + (1, 3)[part])
                if part:
                    need(dve, hlo_last_ready, b - 1)
                nc.vector.tensor_tensor(h_sq[:, c0 * T:c2 * T], h_relu[:, c0 * T:c2 * T], h_relu[:, c0 * T:c2 * T],
                                        ALU.mult).then_inc(hsq_ready, 1)

            def square_low(b, part, n):
                c0, c1 = ((0, 2), (2, low_split(b)))[part]
                dve.wait_ge(hsq_ready, 2 * b + part + 1)
                dve.wait_ge(hhi_ready, 2 * b + part + 1)
                need(dve, ffn_ready, CT * (b - 1))
                nc.vector.tensor_tensor(h_lo[n][:, c0 * T:c1 * T], h_sq[:, c0 * T:c1 * T], h_hi[n][:, c0 * T:c1 * T],
                                        ALU.subtract).then_inc(hlo_ready, 1)

            def weight_scale(n, w0, w1):
                dve.wait_ge(wsums_spread, n)
                step(nc.vector.tensor_scalar(w_root[:, w0:w1].bitcast(U32), bank[7][:, w0:w1].bitcast(U32), 1, EXPONENT,
                                             ALU.logical_shift_right, ALU.bitwise_and))
                step(nc.vector.tensor_scalar(w_range[:, w0:w1], w_root[:, w0:w1], 2.0 ** -100, 2.0 ** 64 / W_SCALE,
                                             ALU.max, ALU.mult))
                nc.vector.reciprocal(w_mul[:, w0:w1], w_range[:, w0:w1]).then_inc(wscale_ready, 1)
                nc.vector.tensor_scalar(unscale[:, w0:w1], w_range[:, w0:w1], 1.0 / X_SCALE, None,
                                        ALU.mult).then_inc(unscale_ready, 1)

            def weight_low(w, e):
                dve.wait_ge(whi_ready, w + 1)
                low, raw, high = (buffer[:, w, :].rearrange("p (c m) -> p c m", c=CD)[:, :, e * P:(e + 1) * P]
                                  for buffer in (w_lo, w_raw, w_hi))
                nc.vector.scalar_tensor_tensor(out=low, in0=raw, scalar=w_mul[:, w:w + 1], in1=high,
                                               op0=ALU.mult, op1=ALU.subtract).then_inc(wlo_ready, 1)

            def ternary_scales():
                dve.wait_ge(fsum_spread, 1)
                step(nc.vector.tensor_scalar(f_mean[:], bank[6][:, 256:258], 1.0 / (D * H), 1e-5, ALU.mult, ALU.max))
                nc.vector.tensor_scalar(f_thr[:], f_mean[:], 0.7, None, ALU.mult)
                step(nc.vector.tensor_tensor(f_mean_sq[:], f_mean[:, 0:1], f_mean[:, 0:1], ALU.mult))
                nc.vector.tensor_scalar(f_nthr[:], f_thr[:], -1.0, None, ALU.mult).then_inc(fthr_ready, 1)
                nc.vector.tensor_scalar(f_unscale[:], f_mean_sq[:], f_mean[:, 1:2], 1.0 / H_SCALE ** 2, ALU.mult,
                                        ALU.mult).then_inc(funscale_ready, 1)

            def columns_of(piece):
                return slice(piece * T, (piece + 1) * T) if isinstance(piece, int) else bass.ds(piece * T, T)

            def below(w, piece):
                dve.wait_ge(fthr_ready, 1)
                nc.vector.tensor_scalar(f_neg[:, w, columns_of(piece)], f_raw[:, w, columns_of(piece)], f_nthr[:, w:w + 1],
                                        None, ALU.is_lt).then_inc(fneg_ready[w], 1)

            def ternary(w, piece):
                where = columns_of(piece)
                dve.wait_ge(fneg_ready[w], piece + 1)
                nc.vector.scalar_tensor_tensor(out=f_q[:, w, where], in0=f_raw[:, w, where], scalar=f_thr[:, w:w + 1],
                                               in1=f_neg[:, w, where], op0=ALU.is_gt, op1=ALU.subtract).then_inc(fq_ready[w], 1)

            def decay_power(c):
                nc.vector.tensor_tensor_scan(d_power[:, c, 1:], d_keep[:, c:c + 1].to_broadcast([P, T - 1]),
                                             zeros[:, 1:], 1e10, ALU.mult, ALU.add).then_inc(dpower_ready, 1)

            def normalise(n, b):
                dve.wait_ge(ln_coef_ready[n], b + 1)
                need(dve, turned[n], b)
                for t in range(CT):
                    nc.vector.tensor_scalar(xn[n][:, t * D:(t + 1) * D], rows(b, t, 1), ln_rs[n][:, t:t + 1],
                                            ln_bias[n][:, t:t + 1], ALU.mult, ALU.add).then_inc(xn_ready[n], 1)

            dve.wait_ge(dsig_ready, 1)
            step(nc.vector.tensor_scalar(d_keep[:], d_sig[:], 1e-7, None, ALU.max))
            dve.wait_ge(consts_ready, 1)
            decay_power(0)
            first_stats(0)
            await_layer_stats(0, 0)
            layer_mean(0, 0)
            dve.wait_ge(ln_mv_ready[0], 1)
            first_stats(1)
            normalise(0, 0)
            weight_scale(1, 0, 3)
            await_layer_stats(0, 1)
            layer_mean(0, 1)
            decay_power(1)
            low_part(0, 0)
            for w in range(2):
                for e in range(CD):
                    weight_low(w, e)
            dve.wait_ge(ln_mv_ready[0], 2)
            first_stats(2)
            await_layer_stats(0, 2)
            layer_mean(0, 2)
            dve.wait_ge(dpower_ready, CD)
            nc.vector.tensor_scalar(kv_weight[:], d_power[:].rearrange("p c t -> p (c t)"), 1.0, unscale[:, 1:2],
                                    ALU.min, ALU.mult).then_inc(kvweight_ready, 1)

            def attention_slot(i):
                at = i if isinstance(i, int) else None
                n, ahead = (0, i + 2) if live(i + 2) else (1, i + 2 - NB)
                if at == 1:
                    dve.wait_ge(in_x[ahead], 16)
                if n == 1:
                    dve.wait_ge(x2_ready, ahead + 1)
                if at != 0:
                    for t in range(CT):
                        layer_stats(n, ahead, t)
                    await_layer_stats(n, ahead)
                if live(i - 2):
                    group_copy(i - 2)
                if at != 0:
                    layer_mean(n, ahead)
                if at == 2:
                    gate_state(1)
                    output_unscale()
                    ternary_scales()
                if at == 0:
                    dve.wait_ge(kvweight_ready, 1)
                    weigh_k(i)
                low_part(*((0, i + 1) if live(i + 1) else (1, 0)))
                if live(i - 2):
                    group_variance(i - 2)
                if at != 0:
                    weigh_k(i)
                if live(i - 2):
                    group_eps(i - 2)
                if live(i - 3):
                    below(0, i - 3)
                    below(1, i - 3)
                kv(i)
                if live(i - 3):
                    ternary(0, i - 3)
                for c in range(CD):
                    scan(i, c)
                if at == 0:
                    weight_scale(2, 3, 5)
                if live(i - 3):
                    ternary(1, i - 3)
                if at == NB - 1:
                    gate_state(at)
                if live(i - 3):
                    add_attention(i - 3)

            def ffn_slot(j, n):
                at = j if isinstance(j, int) else None
                if at == 0:
                    group_copy(NB - 2)
                if at == 1:
                    z_low(NB - 2)
                    add_attention(NB - 3)
                if live(j + 2):
                    dve.wait_ge(x2_ready, NB if at is None else at + 3)
                    layer_stats(1, j + 2, 0)
                    if at == 0:
                        group_variance(NB - 2)
                        group_eps(NB - 2)
                        z_low(NB - 3)
                    layer_stats(1, j + 2, 1)
                    await_layer_stats(1, j + 2)
                if live(j):
                    square(j, 0)
                if live(j + 2):
                    layer_mean(1, j + 2)
                if at == 1:
                    z_low(NB - 1)
                elif at != 0 and live(j):
                    square_low(j, 0, n)
                if live(j + 1):
                    low_part(1, j + 1)
                if at == 0:
                    square_low(j, 0, n)
                    group_copy(NB - 1)
                    group_variance(NB - 1)
                    group_eps(NB - 1)
                if live(j):
                    square(j, 1)
                if at == 1:
                    dve.wait_ge(hlo_ready, 3)
                if live(j):
                    square_low(j, 1, n)
                if at == 1:
                    add_attention(NB - 2)
                    add_attention(NB - 1)
                if at == NB - 1:
                    dve.wait_ge(ffn_ready, CT * (NB - 1))
                    dve.wait_ge(out_ready, NB - 2)
                    nc.vector.scalar_tensor_tensor(out=rows(NB - 2), in0=b_o[:], scalar=f_unscale[:], in1=rows(NB - 2),
                                                   op0=ALU.mult, op1=ALU.add).then_inc(out_ready, 1)
                if at == NB:
                    for t, got in enumerate(last_banks):
                        dve.wait_ge(ffn_ready, CT * (NB - 1) + t + 1)
                        nc.vector.scalar_tensor_tensor(out=rows(NB - 1, t, 1), in0=got, scalar=f_unscale[:],
                                                       in1=rows(NB - 1, t, 1), op0=ALU.mult, op1=ALU.add).then_inc(last_out_ready, 1)

            run_slots(dve, attention_slot, ffn_slot)

        @block.scalar
        def _(act):
            def normalise(n, b):
                act.wait_ge(ln_coef_ready[n], b + 1)
                need(act, turned[n], b)
                for t in range(CT):
                    nc.scalar.activation(xn[n][:, t * D:(t + 1) * D], rows(b, t, 1), ACT.Identity,
                                         bias=ln_bias[n][:, t:t + 1], scale=ln_rs[n][:, t:t + 1]).then_inc(xn_ready[n], 1)

            def high_part(n, b):
                act.wait_ge(turned[n], b + 1)
                nc.scalar.activation(parts(xt_hi[n], b), b_turn[:], ACT.Copy).then_inc(xhi_ready[n], 1)

            def gate_of(b):
                act.wait_ge(r_ready, b + 1)
                need(act, o_ready, b)
                nc.scalar.activation(gate[:], b_r[:], ACT.Sigmoid, scale=unscale[:, 2:3]).then_inc(gate_ready, 1)

            def group_sums(b, which=(0, 1)):
                act.wait_ge(o_ready, b + 1)
                need(act, gn_spread, b)
                for n in which:
                    function = (ACT.Copy, ACT.Square)[n]
                    nc.scalar.activation(gn_copies[n][:], group(b), function,
                                         accum_out=gn_sums[:, n:n + 1]).then_inc(gn_sums_ready, 1)

            def group_normalise(b):
                act.wait_ge(gn_coef_ready, b + 1)
                need(act, zlo_ready, b)
                for c in range(CD):
                    nc.scalar.activation(z_sb[:, c * T:(c + 1) * T], group(b, c, 1), ACT.Identity,
                                         bias=gn_bias[:, c:c + 1], scale=gn_scale[:, c:c + 1]).then_inc(z_ready, 1)

            def z_high(b):
                act.wait_ge(z_ready, CD * (b + 1))
                nc.scalar.activation(parts(z_hi, b), z_of(b)[:], ACT.Copy).then_inc(zhi_ready, 1)

            def relu(b, p):
                h0, h1 = PAIRS[p]
                act.wait_ge(h_ready, 3 * b + p + 1)
                need(act, hsq_ready, 2 * b)
                nc.scalar.activation(h_relu[:, h0 * T:h1 * T], b_h[p][:, 0:(h1 - h0) * T], ACT.Relu,
                                     scale=H_SCALE / X_SCALE).then_inc(relu_ready, 1)

            def square_high(b, part, n):
                c0, c1 = ((0, 2), (2, CH))[part]
                act.wait_ge(relu_ready, 3 * b + (1, 3)[part])
                need(act, ffn_ready, CT * (b - 1))
                nc.scalar.activation(h_hi[n][:, c0 * T:c1 * T], h_relu[:, c0 * T:c1 * T], ACT.Square).then_inc(hhi_ready, 1)

            def copy_ffn(b):
                act.wait_ge(ffn_ready, CT * (b + 1))
                need(act, out_ready, b)
                nc.scalar.activation(ffn_out[:], b_o[:], ACT.Copy, scale=f_unscale[:]).then_inc(ffn_sb_ready, 1)

            def sum_squares(column, src, scale=1.0):
                size = src.shape[1]
                nc.scalar.activation(w_squares[:, column * CD * D:column * CD * D + size], src, ACT.Square, scale=scale,
                                     accum_out=w_sums[:, column:column + 1]).then_inc(wsums_ready, 1)

            def weight_high(w, src):
                nc.scalar.activation(w_hi[:, w, :], src, ACT.Copy, scale=w_mul[:, w:w + 1]).then_inc(whi_ready, 1)

            act.dma_start(cols[:], columns).then_inc(in_cols, 16)
            act.wait_ge(in_cols, 16)
            nc.scalar.activation(d_sig[:], decay_c, ACT.Sigmoid).then_inc(dsig_ready, 1)
            for w in range(3):
                act.wait_ge(in_wqkv[w], 16)
                sum_squares(w, w_raw[:, w, :])
            high_part(0, 0)
            act.wait_ge(wscale_ready, 1)
            weight_high(0, w_raw[:, 0, :])
            weight_high(1, w_raw[:, 1, :])
            normalise(0, 1)
            weight_high(2, w_raw[:, 2, :])
            high_part(0, 1)
            act.wait_ge(in_wout, 16)
            sum_squares(3, w_raw[:, 3, :])
            sum_squares(4, cols[:, CD:3 * CD], scale=Z_MAX * 2.0 ** 0.5)

            def sum_magnitudes(w, half):
                if half == 0:
                    act.wait_ge((in_fc, in_proj)[w], 16)
                where = slice(half * H, (half + 1) * H)
                nc.scalar.activation(f_abs[:, w, where], f_raw[:, w, where], ACT.Abs,
                                     accum_out=f_sum[:, half, w:w + 1]).then_inc(fsum_ready, 1)

            def attention_slot(i):
                at = i if isinstance(i, int) else None
                if at == 0:
                    sum_magnitudes(0, 0)
                elif live(i + 1):
                    high_part(0, i + 1)
                else:
                    high_part(1, 0)
                if at == 1:
                    sum_magnitudes(1, 0)
                if live(i - 3):
                    group_normalise(i - 3)
                    z_high(i - 3)
                if live(i - 1):
                    group_sums(i - 1)
                if live(i + 2):
                    normalise(0, i + 2)
                else:
                    normalise(1, i + 2 - NB)
                gate_of(i)
                if at == 0:
                    sum_magnitudes(0, 1)
                if at == 1:
                    sum_magnitudes(1, 1)
                    act.wait_ge(wscale_ready, 2)
                    weight_high(3, w_raw[:, 3, :])

            def ffn_slot(j, n):
                at = j if isinstance(j, int) else None
                if at == 0:
                    group_sums(NB - 1, (0,))
                    z_high(NB - 3)
                if live(j):
                    relu(j, 0)
                    square_high(j, 0, n)
                if at == 0:
                    high_part(1, 1)
                    group_sums(NB - 1, (1,))
                if live(j):
                    relu(j, 1)
                    relu(j, 2)
                if at == 1:
                    z_high(NB - 1)
                if at != 0 and live(j + 1):
                    high_part(1, j + 1)
                if live(j):
                    square_high(j, 1, n)
                if at == 1:
                    act.wait_ge(funscale_ready, 1)
                    copy_ffn(0)
                if live(j + 2):
                    normalise(1, j + 2)
                if at == 0:
                    z_high(NB - 2)
                if live(j - 1) and at not in (1, NB - 1, NB):
                    copy_ffn(j - 1)

            run_slots(act, attention_slot, ffn_slot)

        @block.gpsimd
        def _(pool):
            def layer_coefficients(n, b):
                need(pool, xn_ready[n], CT * b)
                pool.wait_ge(ln_mv_ready[n], b + 1)
                nc.gpsimd.tensor_tensor(ln_nm[n][:], ln_mv[n][:, :, 0], minus_one[:], ALU.mult).then_inc(ln_step[n], 1)
                nc.gpsimd.tensor_scalar(ln_var[n][:], ln_mv[n][:, :, 1], X_SCALE ** -2, EPS * X_SCALE ** -2,
                                        ALU.mult, ALU.add).then_inc(ln_step[n], 1)
                pool.wait_ge(ln_step[n], 3 * b + 2)
                nc.gpsimd.tensor_tensor(ln_rs[n][:], ln_var[n][:], minus_half[:], ALU.pow).then_inc(ln_step[n], 1)
                pool.wait_ge(ln_step[n], 3 * b + 3)
                nc.gpsimd.tensor_tensor(ln_bias[n][:], ln_nm[n][:], ln_rs[n][:], ALU.mult).then_inc(ln_coef_ready[n], 1)

            def group_coefficients(b):
                need(pool, z_ready, CD * b)
                pool.wait_ge(gn_var_ready, 2 * b + 2)
                nc.gpsimd.tensor_tensor(gn_veps[:], gn_nveps[:], minus_one[:, 0:1], ALU.mult).then_inc(gn_coef_step, 1)
                pool.wait_ge(gn_coef_step, 4 * b + 1)
                nc.gpsimd.tensor_tensor(gn_rs[:], gn_veps[:], minus_half[:, 0:1], ALU.pow).then_inc(gn_coef_step, 1)
                pool.wait_ge(gn_coef_step, 4 * b + 2)
                nc.gpsimd.tensor_tensor(gn_scale[:], gn_wz[:], gn_rs[:].to_broadcast([P, CD]), ALU.mult).then_inc(gn_coef_step, 1)
                pool.wait_ge(gn_coef_step, 4 * b + 3)
                nc.gpsimd.tensor_tensor(gn_shift[:], gn_scale[:], gn_all[:, 0:1].to_broadcast([P, CD]), ALU.mult).then_inc(gn_coef_step, 1)
                pool.wait_ge(gn_coef_step, 4 * b + 4)
                nc.gpsimd.tensor_tensor(gn_bias[:], gn_shift[:], gn_bz[:], ALU.add).then_inc(gn_coef_ready, 1)

            def gate_state(b):
                pool.wait_ge(gate_ready, b + 1)
                pool.wait_ge(scan_ready, CD * (b + 1))
                nc.gpsimd.tensor_tensor(group(b), gate[:], state[:].rearrange("p c t -> p (c t)"), ALU.mult).then_inc(o_ready, 1)

            def group_normalise(b):
                pool.wait_ge(gn_coef_ready, b + 1)
                if z_of(b) is z_sb:
                    pool.wait_ge(zlo_ready, b)
                for c in range(CD):
                    nc.gpsimd.tensor_scalar(z_of(b)[:, c * T:(c + 1) * T], group(b, c, 1), gn_scale[:, c:c + 1],
                                            gn_bias[:, c:c + 1], ALU.mult, ALU.add).then_inc(z_ready, 1)

            def z_low(b):
                pool.wait_ge(zhi_ready, b + 1)
                nc.gpsimd.tensor_tensor(parts(z_lo, b), z_of(b)[:], parts(z_hi, b), ALU.subtract).then_inc(zlo_ready, 1)

            def last_low(b, n):
                pool.wait_ge(hsq_ready, 2 * b + 2)
                pool.wait_ge(hhi_ready, 2 * b + 2)
                need(pool, ffn_ready, CT * (b - 1))
                c = low_split(b) * T
                nc.gpsimd.tensor_tensor(h_lo[n][:, c:], h_sq[:, c:], h_hi[n][:, c:], ALU.subtract).then_inc(hlo_last_ready, 1)

            def first_low(b, n):
                pool.wait_ge(hsq_ready, 2 * b + 1)
                pool.wait_ge(hhi_ready, 2 * b + 1)
                nc.gpsimd.tensor_tensor(h_lo[n][:, 0:2 * T], h_sq[:, 0:2 * T], h_hi[n][:, 0:2 * T],
                                        ALU.subtract).then_inc(hlo_ready, 1)

            def add_ffn(b):
                pool.wait_ge(ffn_sb_ready, b + 1)
                nc.gpsimd.tensor_tensor(rows(b), rows(b), ffn_out[:], ALU.add).then_inc(out_ready, 1)

            def scale_weight(w):
                nc.gpsimd.tensor_scalar(w_scaled[:, w - 2, :], w_raw[:, w, :], w_mul[:, w:w + 1], 0.0, ALU.mult,
                                        ALU.add).then_inc(wscaled_ready, 1)

            def pool_weight_low(w):
                pool.wait_ge(whi_ready, w + 1)
                pool.wait_ge(wscaled_ready, w - 1)
                nc.gpsimd.tensor_tensor(w_lo[:, w, :], w_scaled[:, w - 2, :], w_hi[:, w, :], ALU.subtract).then_inc(wlo_pool_ready, 1)

            nc.gpsimd.memset(ident[:], 0.0).then_inc(consts_step, 1)
            pool.wait_ge(consts_step, 1)
            nc.gpsimd.affine_select(out=ident[:], in_=ident[:], compare_op=ALU.not_equal, fill=1.0, base=0,
                                    pattern=[[-1, P]], channel_multiplier=1)
            nc.gpsimd.memset(minus_half[:], -0.5)
            nc.gpsimd.memset(minus_one[:], -1.0)
            nc.gpsimd.memset(ones[:], 1.0)
            nc.gpsimd.memset(mean_mat[:], -1.0 / (P * N))
            nc.gpsimd.memset(zeros[:], 0.0)
            nc.gpsimd.memset(d_power[:, :, 0:1], 1e10).then_inc(consts_ready, 1)
            pool.wait_ge(consts_ready, 1)
            layer_coefficients(0, 0)
            layer_coefficients(0, 1)
            pool.wait_ge(wscale_ready, 1)
            scale_weight(2)
            pool_weight_low(2)

            def attention_slot(i):
                at = i if isinstance(i, int) else None
                if live(i - 1) and at != 2:
                    gate_state(i - 1)
                if live(i + 2):
                    layer_coefficients(0, i + 2)
                else:
                    layer_coefficients(1, i + 2 - NB)
                if at == 1:
                    pool.wait_ge(wscale_ready, 2)
                    for wide, narrow in ((gn_wz, gn_w_c), (gn_bz, gn_b_c)):
                        nc.gpsimd.tensor_tensor(wide[:], narrow, w_mul[:, 4:5].to_broadcast([P, CD]),
                                                ALU.mult).then_inc(gnaffine_ready, 1)
                    scale_weight(3)
                if at == 2:
                    pool_weight_low(3)
                    pool.wait_ge(gnaffine_ready, 2)
                if live(i - 3):
                    z_low(i - 3)
                if live(i - 2):
                    group_coefficients(i - 2)

            def ffn_slot(j, n):
                at = j if isinstance(j, int) else None
                if at == 0:
                    group_normalise(NB - 3)
                    group_coefficients(NB - 2)
                    layer_coefficients(1, 2)
                    group_normalise(NB - 2)
                if at == 1:
                    group_coefficients(NB - 1)
                    group_normalise(NB - 1)
                    first_low(1, n)
                if at != 0 and live(j + 2):
                    layer_coefficients(1, j + 2)
                if live(j) and at != 0:
                    last_low(j, n)
                if live(j - 1) and at not in (NB - 1, NB):
                    add_ffn(j - 1)

            run_slots(pool, attention_slot, ffn_slot)


def kernel(L0_attn_x, L0_attn_Wr, L0_attn_Wk, L0_attn_Wv, L0_attn_Wo, L0_attn_decay, L0_attn_gn_weight,
           L0_attn_gn_bias, L0_ffn_w_fc, L0_ffn_w_proj):
    import concourse.bacc as bacc
    from concourse.bass_utils import run_bass_kernel_spmd

    def by_partition(a):
        a = np.asarray(a)
        a = a.reshape(a.shape[0] // P, P, -1)
        return np.ascontiguousarray(a.transpose(1, 0, 2).reshape(P, -1))

    B, T, D = L0_attn_x.shape
    arrays = {
        "in_x": by_partition(np.asarray(L0_attn_x).reshape(B * T, D)),
        "in_w_qkv": np.ascontiguousarray(np.concatenate([by_partition(np.asarray(w).T) for w in (L0_attn_Wk, L0_attn_Wv, L0_attn_Wr)], axis=1)),
        "in_w_out": by_partition(np.asarray(L0_attn_Wo).T),
        "in_columns": np.ascontiguousarray(np.concatenate(
            [by_partition(np.asarray(a).reshape(-1, 1)) for a in (L0_attn_decay, L0_attn_gn_weight, L0_attn_gn_bias)], axis=1)),
        "in_w_fc": by_partition(np.asarray(L0_ffn_w_fc).T),
        "in_w_proj": by_partition(np.asarray(L0_ffn_w_proj).T),
    }
    nc = bacc.Bacc("TRN2", target_bir_lowering=False, num_devices=1)
    args = [nc.dram_tensor(n, a.shape, mybir.dt.from_np(a.dtype), kind="ExternalInput").ap() for n, a in arrays.items()]
    result = nc.dram_tensor("result", arrays["in_x"].shape, mybir.dt.float32, kind="ExternalOutput").ap()
    decay_block_kernel(nc, *args, result)
    r = run_bass_kernel_spmd(nc, [arrays], core_ids=[0])
    got = r.results[0]["result"].reshape(P, B * T // P, D)
    return np.ascontiguousarray(got.transpose(1, 0, 2)).reshape(B, T, D)
```
